# Optimizing a Trainium2 kernel written in Bass

```python
import numpy as np
import jax
import jax.numpy as jnp

def _softmax(x, axis=-1):
    return jax.nn.softmax(x, axis=axis)

def _gelu(x):
    return jax.nn.gelu(x, approximate=True)

def _silu(x):
    return jax.nn.silu(x)

def _sigmoid(x):
    return jax.nn.sigmoid(x)

def _layernorm(x, axis=-1, eps=1e-05):
    m = jnp.mean(x, axis=axis, keepdims=True)
    v = jnp.var(x, axis=axis, keepdims=True)
    return (x - m) / jnp.sqrt(v + eps)

def _scatter_add(tgt, idx, src, axis=0):
    return tgt.at[idx].add(src)

def _segment_sum(src, seg, n):
    return jax.ops.segment_sum(src, seg, n)
kernel_name = 'mk_adj_preln_d4_adj_r2_d3ea9e'

def setup_inputs(seed: int=0):
    np.random.seed(seed)
    _w = jnp.asarray

    def _rec_inputs():
        import jax
        import jax.numpy as jnp
        _gk = jax.random.key(seed)
        x = 7.22e-05 + 1 * jax.random.normal(jax.random.fold_in(_gk, 1), (8, 1024, 256), jnp.float32)
        _a = jax.random.bernoulli(jax.random.fold_in(_gk, 2), 0.00390625, (8, 1024, 1024))
        _a = jnp.logical_or(_a, jnp.swapaxes(_a, -1, -2))
        _a = jnp.logical_or(_a, jnp.eye(1024, dtype=bool))
        _af = _a.astype(jnp.float32)
        _af = _af * jax.random.uniform(jax.random.fold_in(_gk, 3), (8, 1024, 1024), jnp.float32, 0.05, 1)
        adj = _af
        return (x, adj)
    x, adj = _rec_inputs()

    def _L0_gnn_setup():
        import jax, jax.numpy as jnp
        import numpy as np
        B, N, D = (8, 1024, 256)
        key = jax.random.key(seed)
        ks = jax.random.split(key, 8)
        scale = 0.5 / np.sqrt(D)
        x = jax.random.normal(ks[0], (B, N, D), dtype=jnp.float32)
        adj = jax.random.uniform(ks[1], (B, N, N), dtype=jnp.float32)
        Wq_w = jax.random.normal(ks[2], (D, D), dtype=jnp.float32) * scale
        Wk_w = jax.random.normal(ks[3], (D, D), dtype=jnp.float32) * scale
        Wv_w = jax.random.normal(ks[4], (D, D), dtype=jnp.float32) * scale
        Wq_b = jnp.zeros((D,), dtype=jnp.float32)
        Wk_b = jnp.zeros((D,), dtype=jnp.float32)
        Wv_b = jnp.zeros((D,), dtype=jnp.float32)
        return {'x': x, 'adj': adj, 'Wq_w': Wq_w, 'Wq_b': Wq_b, 'Wk_w': Wk_w, 'Wk_b': Wk_b, 'Wv_w': Wv_w, 'Wv_b': Wv_b}
    _L0_gnn_all = _L0_gnn_setup()
    _L0_gnn_in = {k: v for k, v in _L0_gnn_all.items() if k in ('Wq_w', 'Wq_b', 'Wk_w', 'Wk_b', 'Wv_w', 'Wv_b')}
    del _L0_gnn_all

    def _L1_gnn_setup():
        import jax, jax.numpy as jnp
        import numpy as np
        key = jax.random.key(seed)
        k1, k2, k3 = jax.random.split(key, 3)
        B, N, F_in, F_out = (64, 62, 256, 256)
        x = jax.random.normal(k1, (B, N, F_in), dtype=jnp.float32)
        adj = jax.random.uniform(k2, (B, N, N), dtype=jnp.float32)
        std = (2.0 / (F_in + F_out)) ** 0.5
        w = jax.random.normal(k3, (F_in, F_out), dtype=jnp.float32) * std
        return {'x': x, 'adj': adj, 'w': w}
    _L1_gnn_all = _L1_gnn_setup()
    _L1_gnn_in = {k: v for k, v in _L1_gnn_all.items() if k in ('w',)}
    del _L1_gnn_all

    def _L2_gnn_setup():
        import jax, jax.numpy as jnp
        import numpy as np
        EPS = 1e-06
        key = jax.random.key(seed)
        k1, k2, k3 = jax.random.split(key, 3)
        B, N, F, O = (8, 2048, 256, 256)
        x = jax.random.normal(k1, (B, N, F), dtype=jnp.float32)
        adj = jax.random.uniform(k2, (B, N, N), dtype=jnp.float32)
        W = jax.random.normal(k3, (O, 2 * F), dtype=jnp.float32) * (1.0 / np.sqrt(2 * F))
        return {'x': x, 'adj': adj, 'W': W}
    _L2_gnn_all = _L2_gnn_setup()
    _L2_gnn_in = {k: v for k, v in _L2_gnn_all.items() if k in ('W',)}
    del _L2_gnn_all

    def _L3_gnn_setup():
        import jax, jax.numpy as jnp
        import numpy as np
        B, N, DIN, DOUT, K = (4, 1024, 256, 256, 3)
        key = jax.random.key(seed)
        ks = jax.random.split(key, 8)
        X = jax.random.normal(ks[0], (B, N, DIN), dtype=jnp.float32)
        A = jax.random.uniform(ks[1], (B, N, N), dtype=jnp.float32)
        Wv = jax.random.normal(ks[2], (DIN, DOUT), dtype=jnp.float32) * 0.02
        bv = jax.random.normal(ks[3], (DOUT,), dtype=jnp.float32) * 0.02
        aw = jax.random.normal(ks[4], (2 * DOUT, 1), dtype=jnp.float32) * 0.05
        ab = jax.random.normal(ks[5], (1,), dtype=jnp.float32) * 0.05
        Wk = jax.random.normal(ks[6], (K, DIN, DOUT), dtype=jnp.float32) * 0.02
        bk = jax.random.normal(ks[7], (K, DOUT), dtype=jnp.float32) * 0.02
        return {'X': X, 'A': A, 'Wv': Wv, 'bv': bv, 'aw': aw, 'ab': ab, 'Wk': Wk, 'bk': bk}
    _L3_gnn_all = _L3_gnn_setup()
    _L3_gnn_in = {k: v for k, v in _L3_gnn_all.items() if k in ('Wv', 'bv', 'aw', 'ab', 'Wk', 'bk')}
    del _L3_gnn_all
    return {'x': x, 'adj': adj, 'L0_gnn_Wq_w': _L0_gnn_in['Wq_w'], 'L0_gnn_Wq_b': _L0_gnn_in['Wq_b'], 'L0_gnn_Wk_w': _L0_gnn_in['Wk_w'], 'L0_gnn_Wk_b': _L0_gnn_in['Wk_b'], 'L0_gnn_Wv_w': _L0_gnn_in['Wv_w'], 'L0_gnn_Wv_b': _L0_gnn_in['Wv_b'], 'L1_gnn_w': _L1_gnn_in['w'], 'L2_gnn_W': _L2_gnn_in['W'], 'L3_gnn_Wv': _L3_gnn_in['Wv'], 'L3_gnn_bv': _L3_gnn_in['bv'], 'L3_gnn_aw': _L3_gnn_in['aw'], 'L3_gnn_ab': _L3_gnn_in['ab'], 'L3_gnn_Wk': _L3_gnn_in['Wk'], 'L3_gnn_bk': _L3_gnn_in['bk']}

def reference(x, adj, L0_gnn_Wq_w, L0_gnn_Wq_b, L0_gnn_Wk_w, L0_gnn_Wk_b, L0_gnn_Wv_w, L0_gnn_Wv_b, L1_gnn_w, L2_gnn_W, L3_gnn_Wv, L3_gnn_bv, L3_gnn_aw, L3_gnn_ab, L3_gnn_Wk, L3_gnn_bk):
    import jax
    import jax.numpy as jnp

    def _L0_gnn_ref(x, adj, Wq_w, Wq_b, Wk_w, Wk_b, Wv_w, Wv_b):
        import jax, jax.numpy as jnp
        import numpy as np
        B, N, D = (8, 1024, 256)
        query = jnp.einsum('bnd,od->bno', x, Wq_w) + Wq_b
        keyt = jnp.einsum('bnd,od->bno', x, Wk_w) + Wk_b
        value = jnp.einsum('bnd,od->bno', x, Wv_w) + Wv_b
        weight = jnp.einsum('bqd,bkd->bqk', query, keyt)
        weight = adj * jnp.exp(weight)
        weight = weight / jnp.sum(weight, axis=2, keepdims=True)
        return jnp.einsum('bqk,bkd->bqd', weight, value)

    def _L1_gnn_ref(x, adj, w):
        import jax, jax.numpy as jnp
        import numpy as np
        agg = jnp.einsum('bnm,bmf->bnf', adj, x)
        return jnp.einsum('bnf,fo->bno', agg, w)

    def _L2_gnn_ref(x, adj, W):
        import jax, jax.numpy as jnp
        import numpy as np
        EPS = 1e-06
        deg = jnp.sum(adj, axis=-1, keepdims=True)
        agg = jnp.einsum('bij,bjf->bif', adj, x) / jnp.maximum(deg, EPS)
        cat = jnp.concatenate([x, agg], axis=2)
        out = jnp.einsum('bnf,of->bno', cat, W)
        return jax.nn.relu(out)

    def _L3_gnn_ref(X, A, Wv, bv, aw, ab, Wk, bk):
        import jax, jax.numpy as jnp
        import numpy as np
        B, N, DIN, DOUT, K = (4, 1024, 256, 256, 3)
        d = Wv.shape[1]
        Xw = X @ Wv + bv
        sj = Xw @ aw[:d, 0]
        si = Xw @ aw[d:, 0]
        e = jax.nn.leaky_relu(sj[:, None, :] + si[:, :, None] + ab[0], negative_slope=0.2)
        alpha_matrix = A * jnp.exp(e)
        transition = alpha_matrix / (jnp.sum(alpha_matrix, axis=-1, keepdims=True) + 1e-12)
        H = jnp.zeros(X.shape[:-1] + (d,), dtype=X.dtype)
        Xk = X
        for k in range(Wk.shape[0]):
            H = H + Xk @ Wk[k] + bk[k]
            Xk = jnp.einsum('bij,bjd->bid', transition, Xk)
        return jax.nn.relu(H)
    h = jnp.maximum(_layernorm(x, axis=-1), 0.0)
    x = x + _L0_gnn_ref(h, adj, L0_gnn_Wq_w, L0_gnn_Wq_b, L0_gnn_Wk_w, L0_gnn_Wk_b, L0_gnn_Wv_w, L0_gnn_Wv_b)
    h = jnp.maximum(_layernorm(x, axis=-1), 0.0)
    x = x + _L1_gnn_ref(h, adj, L1_gnn_w)
    h = jnp.maximum(_layernorm(x, axis=-1), 0.0)
    x = x + _L2_gnn_ref(h, adj, L2_gnn_W)
    h = jnp.maximum(_layernorm(x, axis=-1), 0.0)
    x = x + _L3_gnn_ref(h, adj, L3_gnn_Wv, L3_gnn_bv, L3_gnn_aw, L3_gnn_ab, L3_gnn_Wk, L3_gnn_bk)
    return x

_drawn_inputs = setup_inputs


def setup_inputs(seed=0):
    import zlib

    import numpy as np

    out = dict(_drawn_inputs(seed))
    spreads = {'L0_gnn_Wq_b': (0.0, 0.1), 'L0_gnn_Wk_b': (0.0, 0.8), 'L0_gnn_Wv_b': (0.0, 0.1)}
    factors = {'L3_gnn_Wv': 8.0, 'L3_gnn_bv': 8.0, 'L3_gnn_aw': 8.0, 'L3_gnn_bk': 6.235}
    for name, (base, spread) in spreads.items():
        noise = np.random.default_rng([zlib.crc32(name.encode()), seed]).standard_normal(out[name].shape)
        drawn = base * np.exp(spread * noise) if base else spread * noise
        out[name] = jnp.asarray(drawn.astype(out[name].dtype))
    for name, factor in factors.items():
        out[name] = (out[name] * factor).astype(out[name].dtype)
    return out
```

```python
from contextlib import ExitStack

import concourse.bass as bass
from concourse import mybir

F32 = mybir.dt.float32
F32R = mybir.dt.float32r
ALU = mybir.AluOpType
ACT = mybir.ActivationFunctionType

P = 128
B, N, D = 8, 1024, 256
NB = N // P
FB = D // P
CH = 512
BPC = CH // P
NT = NB * (N // CH)
RW = D + 2
ACCS = 4
S_BANK, PJ_BANK, TR_BANK = 4, 6, 7
RING = 3
LN_EPS, DEG_EPS, SUM_EPS = 1e-5, 1e-6, 1e-12

LNS = 4 * NB
RES = 5 * NB
L0, L1, L2, L3A, L3B = (NB * k for k in range(5))


def gnn_program(nc, x_d, adjT_d, Wq_d, Wk_d, bq_d, bk_d, WvT_d, bv_d, w1_d, w2_d,
                wv3T_d, bv3_d, aw_d, ab_d, wk2_d, wk10_d, bk3_d, out_d):
    ctx = ExitStack()
    with ctx:
        def sb(name, shape, dt=F32):
            return ctx.enter_context(nc.sbuf_tensor(name, shape, dt))

        def sem(name):
            return ctx.enter_context(nc.semaphore(name))

        KB = 1024
        base = -(-nc.sbuf_base // 32) * 32
        sb("slab", [P, 108 * KB // 4])

        def at(name, shape, dt, off):
            return nc.alloc_sbuf_tensor_at(name, shape, dt, offset=base + off)

        a_hi = at("a_hi", [P, NB, N], F32R, 0)
        a_lo = at("a_lo", [P, NB, N], F32R, 32 * KB)
        a_work = at("a_work", [P, NB, N], F32, 32 * KB)
        t_hi = at("t_hi", [P, FB, N], F32R, 64 * KB)
        t_lo = at("t_lo", [P, FB, N], F32R, 72 * KB)
        g1 = at("g1", [P, NB, D], F32, 64 * KB)
        si = at("si", [P, N], F32, 72 * KB)
        si2 = at("si2", [P, N], F32, 76 * KB)
        p_hi = at("p_hi", [P, RING, CH], F32R, 80 * KB)
        p_lo = at("p_lo", [P, RING, CH], F32R, 86 * KB)
        p_work = at("p_work", [P, RING, CH], F32, 86 * KB)
        own = at("own", [P, NB, D], F32, 80 * KB)
        ht_hi = at("ht_hi", [P, FB, N], F32R, 92 * KB)
        ht_lo = at("ht_lo", [P, FB, N], F32R, 100 * KB)
        wq_raw = at("wq_raw", [P, FB, D], F32, 0)
        wk_raw = at("wk_raw", [P, FB, D], F32, 2 * KB)
        wv_raw = at("wv_raw", [P, FB, D], F32, 4 * KB)
        w1_raw = at("w1_raw", [P, FB, D], F32, 6 * KB)
        wv3_raw = at("wv3_raw", [P, FB, D], F32, 8 * KB)
        wk2_raw = at("wk2_raw", [P, FB, D], F32, 10 * KB)
        w2_raw = at("w2_raw", [P, FB, 2 * D], F32, 12 * KB)
        wk10_raw = at("wk10_raw", [P, FB, 2 * D], F32, 16 * KB)
        bk3_raw = at("bk3_raw", [P, 3, D], F32, 20 * KB)
        bq_raw = at("bq_raw", [P, FB], F32, 23 * KB)
        bk_raw = at("bk_raw", [P, FB], F32, 23 * KB + 32)
        bv3_raw = at("bv3_raw", [P, FB], F32, 23 * KB + 64)
        aw_raw = at("aw_raw", [P, 2, FB], F32, 23 * KB + 96)
        ab_raw = at("ab_raw", [P, 1], F32, 23 * KB + 128)
        bb = at("bb", [P, 2, FB], F32, 23 * KB + 160)
        aws = at("aws", [P, FB], F32, 23 * KB + 192)
        urow = at("urow", [P, FB, 4], F32, 23 * KB + 224)
        ui_full = at("ui_full", [P, FB, P], F32, 24 * KB)
        sums = at("sums", [P, 2], F32, 25 * KB)
        bk_two = at("bk_two", [P, D], F32, 26 * KB)

        x_in = sb("x_in", [P, NB, D])
        x = sb("x", [P, NB, D])
        r_hi = [sb(f"r{k}_hi", [P, NB, RW], F32R) for k in range(2)]
        r_lo = [sb(f"r{k}_lo", [P, NB, RW], F32R) for k in range(2)]
        adj_in = sb("adj_in", [P, 2, 2, CH])
        wm = [sb(f"wm_{s}", [P, FB, D], F32R) for s in ("hi", "lo")]
        wv = [sb(f"wv_{s}", [P, FB, RW], F32R) for s in ("hi", "lo")]
        w1 = [sb(f"w1_{s}", [P, FB, D], F32R) for s in ("hi", "lo")]
        w2 = [sb(f"w2_{s}", [P, FB, 2 * D], F32R) for s in ("hi", "lo")]
        wk2 = [sb(f"wk2_{s}", [P, FB, RW], F32R) for s in ("hi", "lo")]
        wk10 = [sb(f"wk10_{s}", [P, FB, 2 * D], F32R) for s in ("hi", "lo")]
        wui = [sb(f"wui_{s}", [P, FB, P], F32R) for s in ("hi", "lo")]
        bv_row = sb("bv_row", [P, D])
        bk_row = sb("bk_row", [P, D])
        h = sb("h", [P, 2, D])
        u = sb("u", [P, 2, D])
        ident = sb("ident", [P, P])
        bn = sb("bn", [P, NB, 6])
        mv = sb("mv", [P, NB, 2])
        ve = sb("ve", [P, NB])
        rstd = sb("rstd", [P, NB])
        nmr = sb("nmr", [P, NB])
        minus_half = sb("minus_half", [P, 1])
        tc = sb("tc", [P, FB])
        g0 = sb("g0", [P, 1])
        s0 = sb("s0", [P, 1])
        g = sb("g", [P, NB])
        sj8 = sb("sj8", [P, NB])
        sj2 = sb("sj2", [P, NB])
        den = sb("den", [P, NB])
        rden = sb("rden", [P, NB])
        ps = ctx.enter_context(nc.psum_tensor("ps", [P, 8, CH], F32))

        passed_sp, passed_v, passed_p = sem("passed_sp"), sem("passed_v"), sem("passed_p")
        w_loaded, x_loaded, stored = sem("w_loaded"), sem("x_loaded"), sem("stored")
        adj_loaded = [sem("adj_loaded0"), sem("adj_loaded1")]
        setup_v, setup_p, setup_pe = sem("setup_v"), sem("setup_p"), sem("setup_pe")
        bn_done, mv_done = sem("bn_done"), sem("mv_done")
        ve_done, rstd_done, nmr_done = sem("ve_done"), sem("rstd_done"), sem("nmr_done")
        xb_done = sem("xb_done")
        h_done, hthi_done = sem("h_done"), sem("hthi_done")
        tr_done = sem("tr_done")
        htlo_done = sem("htlo_done")
        pj_done, rhi_done, rlo_done = sem("pj_done"), sem("rhi_done"), sem("rlo_done")
        tp_done, thi_done, tlo_done = sem("tp_done"), sem("thi_done"), sem("tlo_done")
        s_done, exp_done, mul_done = sem("s_done"), sem("exp_done"), sem("mul_done")
        phi_done, plo_done, pv_done = sem("phi_done"), sem("plo_done"), sem("pv_done")
        ahi_done, alo_done = sem("ahi_done"), sem("alo_done")
        res_done, res_read = sem("res_done"), sem("res_read")
        den_done, rden_done, x2_done, out_done = sem("den_done"), sem("rden_done"), sem("x2_done"), sem("out_done")
        si_done, si_read = sem("si_done"), sem("si_read")
        relu_done, add_done, e3_done = sem("relu_done"), sem("add_done"), sem("e3_done")
        mul3_done, whi_done, wlo_done = sem("mul3_done"), sem("whi_done"), sem("wlo_done")
        gh_done, g1_done, own_done = sem("gh_done"), sem("g1_done"), sem("own_done")
        ghi_done, glo_done = sem("ghi_done"), sem("glo_done")

        SETUP_BB = 2 + 2 + 1 + 2 * 5 + 5 + 2
        SETUP_V = SETUP_BB + FB * (2 * 3 + 3 + 2) + 4
        R_OF = {L0: 0, L1: 1, L2: 0, L3A: 1, L3B: 0}
        N_W = 15

        def blk(j):
            return slice(j * P, (j + 1) * P)

        def chunk(c):
            return slice(c * CH, (c + 1) * CH)

        block = ctx.enter_context(nc.Block())

        @block.sync
        def _(sp):
            def halves(w):
                return w.rearrange("(a p) n -> p a n", p=P)
            for dst, src in (
                (wq_raw[:], halves(Wq_d)), (wk_raw[:], halves(Wk_d)), (wv_raw[:], halves(WvT_d)),
                (w1_raw[:], halves(w1_d)), (wv3_raw[:], halves(wv3T_d)), (wk2_raw[:], halves(wk2_d)),
                (w2_raw[:], halves(w2_d)), (wk10_raw[:], halves(wk10_d)),
                (bk3_raw[:], bk3_d.partition_broadcast(P)), (bv_row[:], bv_d.partition_broadcast(P)),
                (bq_raw[:], bq_d), (bk_raw[:], bk_d), (bv3_raw[:], bv3_d), (aw_raw[:], aw_d),
                (ab_raw[:], ab_d.partition_broadcast(P)),
            ):
                sp.dma_start(dst, src).then_inc(w_loaded, 16)

            def load_x(i):
                sp.dma_start(x_in[:], x_d[bass.ds(i, 1)].rearrange("b (j p) d -> p (b j) d", p=P)
                             if not isinstance(i, int) else
                             x_d[i].rearrange("(j p) d -> p j d", p=P)).then_inc(x_loaded, 16)

            def load_adj(i, s):
                c, pair = s % 8 // 4, s % 4
                src = adjT_d[i] if isinstance(i, int) else adjT_d[bass.ds(i, 1)]
                if isinstance(i, int):
                    src = src.rearrange("(a m p) n -> a p m n", m=2, p=P)[pair][:, :, chunk(c)]
                else:
                    src = src.rearrange("b (a m p) n -> a p (b m) n", m=2, p=P)[pair][:, :, chunk(c)]
                sp.dma_start(adj_in[:, s % 2], src).then_inc(adj_loaded[s % 2], 16)

            def freed(i, s):
                if s <= 9:
                    sp.wait_ge(mul_done, i * NT + 2 * (s - 1))
                    sp.wait_ge(alo_done, i * NT + 2 * (s - 1))
                else:
                    sp.wait_ge(mul3_done, i * NT + 2 * (s - 9))
                sp.sem_inc(passed_sp, 1)

            def graph(i, more):
                for s in range(2, 8):
                    freed(i, s)
                    load_adj(i, s)
                if more:
                    sp.wait_ge(res_read, i * RES + L1)
                    sp.sem_inc(passed_sp, 1)
                    load_x(i + 1)
                for s in range(8, 16):
                    freed(i, s)
                    load_adj(i, s)
                if more:
                    for s in range(16, 18):
                        freed(i, s)
                        load_adj(i + 1, s - 16)

            load_x(0)
            for s in range(2):
                load_adj(0, s)
            with sp.Fori(0, B - 1) as i:
                graph(i, True)
            graph(B - 1, False)

        @block.gpsimd
        def _(pool):
            gp = nc.gpsimd
            gp.memset(ident[:], 0.0).then_inc(setup_p, 1)
            gp.memset(minus_half[:], -0.5).then_inc(setup_p, 1)
            pool.wait_ge(setup_p, 2)
            gp.affine_select(out=ident[:], in_=ident[:], compare_op=ALU.not_equal, fill=1.0, base=0,
                             pattern=[[-1, P]], channel_multiplier=1).then_inc(setup_p, 1)
            pool.wait_ge(w_loaded, 16 * N_W)

            def rstds(i, l, j):
                q = l * NB + j + 1
                pool.wait_ge(mv_done, i * LNS + q)
                pool.sem_inc(passed_p, 1)
                gp.tensor_scalar(ve[:, j:j + 1], mv[:, j, 1:2], LN_EPS, 1.0, ALU.add, ALU.mult).then_inc(ve_done, 1)
                pool.wait_ge(ve_done, i * LNS + q)
                gp.tensor_tensor(rstd[:, j:j + 1], ve[:, j:j + 1], minus_half[:], ALU.pow).then_inc(rstd_done, 1)
                pool.wait_ge(rstd_done, i * LNS + q)
                pool.sem_inc(passed_p, 1)
                gp.tensor_scalar(nmr[:, j:j + 1], mv[:, j, 0:1], rstd[:, j:j + 1], -1.0,
                                 ALU.mult, ALU.mult).then_inc(nmr_done, 1)

            def split_adj(i, t):
                c, m = divmod(t, NB)
                pool.wait_ge(ahi_done, i * NT + t + 1)
                gp.tensor_tensor(a_lo[:, m, chunk(c)], adj_in[:, t // 2 % 2, t % 2],
                                 a_hi[:, m, chunk(c)].bitcast(F32), ALU.subtract).then_inc(alo_done, 1)

            def add3(i, t):
                c, m = divmod(t, NB)
                pool.wait_ge(relu_done, i * NT + t + 1)
                gp.tensor_tensor(a_work[:, m, chunk(c)], a_work[:, m, chunk(c)], si2[:, chunk(c)],
                                 ALU.add).then_inc(add_done, 1)

            def split_g(i, j):
                pool.wait_ge(ghi_done, i * NB + j + 1)
                gp.tensor_tensor(r_lo[0][:, j, 0:D], g1[:, j], r_hi[0][:, j, 0:D].bitcast(F32),
                                 ALU.subtract).then_inc(glo_done, 1)

            with pool.Fori(0, B) as i:
                for j in range(NB):
                    rstds(i, 0, j)
                for j in range(NB):
                    pool.wait_ge(h_done, i * LNS + j + 1)
                    gp.tensor_tensor(x_in[:, j], x_in[:, j], bv_row[:], ALU.add).then_inc(xb_done, 1)
                for t in range(NT):
                    split_adj(i, t)
                    if t in (8, 9, 10, 11):
                        rstds(i, 1, t - 8)
                for j in range(BPC, NB):
                    rstds(i, 1, j)
                for l in (2, 3):
                    for j in range(NB):
                        rstds(i, l, j)
                for t in range(NT):
                    add3(i, t)
                    if t == 13:
                        for j in range(BPC):
                            split_g(i, j)
                for j in range(BPC, NB):
                    split_g(i, j)

        @block.scalar
        def _(act):
            sc = nc.scalar

            def norm(i, l, j):
                q = l * NB + j + 1
                act.wait_ge(nmr_done, i * LNS + q)
                if q > 2:
                    act.wait_ge(tr_done, i * LNS + q - 2)
                src = x_in if l == 0 else x
                sc.activation(h[:, j % 2], src[:, j], ACT.Relu, bias=nmr[:, j:j + 1],
                              scale=rstd[:, j:j + 1]).then_inc(h_done, 1)

            def ht(i, l, j):
                act.wait_ge(tr_done, i * LNS + l * NB + j + 1)
                sc.copy(ht_hi[:, :, blk(j)],
                        ps[:, TR_BANK, 0:D].rearrange("p (a n) -> p a n", a=FB)).then_inc(hthi_done, 1)

            def right(i, l, j):
                k = l % 2
                act.wait_ge(pj_done, i * LNS + l * NB + j + 1)
                if l == 2:
                    sc.copy(own[:, j], ps[:, PJ_BANK, D:2 * D])
                sc.copy(r_hi[k][:, j, 0:D], ps[:, PJ_BANK, 0:D]).then_inc(rhi_done, 1)

            def t_split(i, v):
                db, c = v // 2, v % 2
                act.wait_ge(tp_done, i * 4 + v + 1)
                sc.activation(t_hi[:, db, chunk(c)], ps[:, S_BANK + v % 2], ACT.Identity,
                              bias=tc[:, db:db + 1]).then_inc(thi_done, 1)

            def weighed(i, t):
                c, m = divmod(t, NB)
                if m == NB - 1:
                    act.wait_ge(res_done, i * RES + (c + 1) * BPC)
                else:
                    act.wait_ge(pv_done, i * (NT - 2) + t - c + 1)

            def expo(i, t):
                m = t % NB
                act.wait_ge(s_done, i * NT + t + 1)
                if t >= RING:
                    weighed(i, t - RING)
                sc.activation(p_work[:, t % RING], ps[:, S_BANK + t % 2], ACT.Exp,
                              bias=g[:, m:m + 1]).then_inc(exp_done, 1)

            def p_split(i, t):
                act.wait_ge(mul_done, i * NT + t + 1)
                sc.copy(p_hi[:, t % RING], p_work[:, t % RING]).then_inc(phi_done, 1)

            def relu3(i, t):
                c, m = divmod(t, NB)
                if t == 0:
                    act.wait_ge(rlo_done, i * LNS + LNS)
                    act.wait_ge(si_read, i * 4 + 4)
                sc.activation(a_work[:, m, chunk(c)], si[:, chunk(c)], ACT.Relu, scale=0.8,
                              bias=sj8[:, m:m + 1]).then_inc(relu_done, 1)

            def exp3(i, t):
                c, m = divmod(t, NB)
                act.wait_ge(add_done, i * NT + t + 1)
                sc.activation(a_work[:, m, chunk(c)], a_work[:, m, chunk(c)], ACT.Exp,
                              bias=sj2[:, m:m + 1]).then_inc(e3_done, 1)

            def w_split(i, t):
                c, m = divmod(t, NB)
                act.wait_ge(mul3_done, i * NT + t + 1)
                sc.copy(a_hi[:, m, chunk(c)], a_work[:, m, chunk(c)]).then_inc(whi_done, 1)

            def g1_copy(i, k):
                act.wait_ge(gh_done, i * NB + k + 1)
                sc.copy(g1[:, k], ps[:, S_BANK + k % 2, 0:D]).then_inc(g1_done, 1)

            def g_split(i, j):
                act.wait_ge(res_read, i * RES + L3A + j + 1)
                sc.copy(r_hi[0][:, j, 0:D], g1[:, j]).then_inc(ghi_done, 1)

            act.wait_ge(setup_v, SETUP_V)
            AFTER = {8: [(norm, 0), (norm, 1)], 9: [(ht, 0)], 10: [(norm, 2), (ht, 1)],
                     11: [(norm, 3), (right, 0)], 12: [(ht, 2), (right, 1)],
                     13: [(ht, 3), (right, 2)], 14: [(right, 3)]}
            with act.Fori(0, B) as i:
                for k in range(NB + 2):
                    if k < NB:
                        norm(i, 0, k)
                    if 0 <= k - 1 < NB:
                        ht(i, 0, k - 1)
                    if k >= 2:
                        right(i, 0, k - 2)
                for v in range(4):
                    t_split(i, v)
                expo(i, 0)
                for t in range(NT):
                    if t + 1 < NT:
                        expo(i, t + 1)
                    p_split(i, t)
                    for what, j in AFTER.get(t, ()):
                        what(i, 1, j)
                for l in (1, 2, 3):
                    first = BPC if l == 1 else 0
                    for k in range(first, NB + 2):
                        if k < NB:
                            norm(i, l, k)
                        if first <= k - 1 < NB:
                            ht(i, l, k - 1)
                        if k - 2 >= first:
                            right(i, l, k - 2)
                for c in range(2):
                    act.wait_ge(si_done, i * 2 + c + 1)
                    sc.copy(si[:, chunk(c)], ps[:, S_BANK + c]).then_inc(si_read, 1)
                    sc.mul(si2[:, chunk(c)], ps[:, S_BANK + c], 0.2).then_inc(si_read, 1)
                for t in range(3):
                    relu3(i, t)
                g1_copy(i, 0)
                for t in range(NT + 1):
                    if t < NT:
                        exp3(i, t)
                    if t:
                        w_split(i, t - 1)
                    if t + 3 < NT:
                        relu3(i, t + 3)
                    if t + 1 < NB:
                        g1_copy(i, t + 1)
                    if t == 10:
                        for j in range(BPC):
                            g_split(i, j)
                for j in range(BPC, NB):
                    g_split(i, j)
                for c in range(2):
                    act.wait_ge(out_done, i * NB + (c + 1) * BPC)
                    act.dma_start(out_d[bass.ds(i, 1)].rearrange("b (c j p) d -> c p (b j) d", c=2, p=P)[c],
                                  x[:, c * BPC:(c + 1) * BPC]).then_inc(stored, 16)
            act.wait_ge(stored, 16 + 32 * B)

        @block.vector
        def _(dve):
            ve_ = nc.vector
            steps = [0]

            def link(ins):
                steps[0] += 1
                ins.then_inc(setup_v, 1)
                dve.wait_ge(setup_v, steps[0])

            def split(pair, dst, src):
                link(ve_.tensor_copy(dst(pair[0]), src))
                link(ve_.tensor_tensor(dst(pair[1]), src, dst(pair[0]).bitcast(F32), ALU.subtract))

            for k in range(2):
                ve_.memset(r_hi[k][:, :, D:D + 1].bitcast(F32), 1.0)
                ve_.memset(r_hi[k][:, :, D + 1:RW].bitcast(F32), 0.0)
                link(ve_.memset(r_lo[k][:, :, D:RW].bitcast(F32), 0.0))
            for w in wv + wk2:
                link(ve_.memset(w[:, :, D:RW].bitcast(F32), 0.0))
            link(ve_.memset(ui_full[:], 1.0))
            dve.wait_ge(w_loaded, 16 * N_W)
            for pair, raw in ((wv, wv_raw), (w1, w1_raw), (wk2, wk2_raw)):
                split(pair, lambda w: w[:, :, 0:D], raw[:])
            for pair, raw in ((w2, w2_raw), (wk10, wk10_raw)):
                split(pair, lambda w: w[:], raw[:])
            link(ve_.tensor_tensor(bk_two[:], bk3_raw[:, 0], bk3_raw[:, 1], ALU.add))
            link(ve_.tensor_tensor(bk_row[:], bk_two[:], bk3_raw[:, 2], ALU.add))
            link(ve_.tensor_tensor(bb[:, 0], bq_raw[:], bk_raw[:], ALU.mult))
            link(ve_.tensor_tensor(aws[:], aw_raw[:, 0], aw_raw[:, 1], ALU.add))
            link(ve_.tensor_tensor(bb[:, 1], bv3_raw[:], aws[:], ALU.mult))
            assert steps[0] == SETUP_BB
            dve.wait_ge(setup_pe, 1)
            for fb in range(FB):
                split(wm, lambda w: w[:, fb], ps[:, fb, 0:D])
                split(wv, lambda w: w[:, fb, D:D + 1], ps[:, 2 + fb, 0:1])
                split(wk2, lambda w: w[:, fb, D:D + 1], ps[:, 2 + fb, 2:3])
                link(ve_.tensor_copy(tc[:, fb:fb + 1], ps[:, 2 + fb, 1:2]))
                link(ve_.tensor_copy(urow[:, fb, 0:1], ps[:, 2 + fb, 3:4]))
                link(ve_.tensor_scalar(ui_full[:, fb], ui_full[:, fb], urow[:, fb, 0:1], None, ALU.mult))
                split(wui, lambda w: w[:, fb], ui_full[:, fb])
            link(ve_.tensor_copy(sums[:, 0:1], ps[:, 4, 0:1]))
            link(ve_.tensor_copy(sums[:, 1:2], ps[:, 4, 1:2]))
            link(ve_.tensor_copy(g0[:], sums[:, 0:1]))
            link(ve_.tensor_tensor(s0[:], sums[:, 1:2], ab_raw[:], ALU.add))
            ve_.memset(u[:, 0, 0:1], 0.0).then_inc(stored, 16)
            assert steps[0] == SETUP_V, steps[0]

            def stats(i, l, j):
                q = l * NB + j + 1
                if l == 0 and j == 0:
                    dve.wait_ge(x_loaded, i * 16 + 16)
                if l:
                    dve.wait_ge(*x_ready(i, l, j))
                src = x_in if l == 0 else x
                ve_.bn_stats(bn[:, j], src[:, j]).then_inc(bn_done, 1)
                dve.wait_ge(bn_done, i * LNS + q)
                dve.sem_inc(passed_v, 1)
                ve_.bn_aggr(mv[:, j], bn[:, j]).then_inc(mv_done, 1)

            def x_ready(i, l, j):
                if l == 3:
                    return x2_done, i * NB + j + 1
                return res_read, i * RES + (l - 1) * NB + j + 1

            def ht(i, l, j):
                dve.wait_ge(hthi_done, i * LNS + l * NB + j + 1)
                ve_.tensor_tensor(ht_lo[:, :, blk(j)], ps[:, TR_BANK, 0:D].rearrange("p (a n) -> p a n", a=FB),
                                  ht_hi[:, :, blk(j)].bitcast(F32), ALU.subtract).then_inc(htlo_done, 1)

            def right(i, l, j):
                k = l % 2
                dve.wait_ge(rhi_done, i * LNS + l * NB + j + 1)
                last = ps[:, PJ_BANK, D:D + 1]
                if l == 0:
                    ve_.tensor_scalar(g[:, j:j + 1], last, g0[:], None, ALU.add)
                if l == 3:
                    ve_.tensor_scalar(sj8[:, j:j + 1], last, s0[:], 0.8, ALU.add, ALU.mult)
                    ve_.tensor_scalar(sj2[:, j:j + 1], last, s0[:], 0.2, ALU.add, ALU.mult)
                ve_.tensor_tensor(r_lo[k][:, j, 0:D], ps[:, PJ_BANK, 0:D],
                                  r_hi[k][:, j, 0:D].bitcast(F32), ALU.subtract).then_inc(rlo_done, 1)

            def res0(i, j):
                dve.wait_ge(res_done, i * RES + L0 + j + 1)
                ve_.reciprocal(rden[:, j:j + 1], ps[:, j % ACCS, D:D + 1]).then_inc(rden_done, 1)
                if j == 0:
                    dve.wait_ge(stored, i * 32 + 16)
                dve.wait_ge(xb_done, i * NB + j + 1)
                dve.wait_ge(rden_done, i * 3 * NB + j + 1)
                ve_.scalar_tensor_tensor(out=x[:, j], in0=ps[:, j % ACCS, 0:D], scalar=rden[:, j:j + 1],
                                         in1=x_in[:, j], op0=ALU.mult, op1=ALU.add).then_inc(res_read, 1)

            def res1(i, j):
                dve.wait_ge(res_done, i * RES + L1 + j + 1)
                ve_.tensor_tensor(x[:, j], ps[:, j % ACCS, 0:D], x[:, j], ALU.add).then_inc(res_read, 1)

            def divide(i, a, j, op, eps, k):
                dve.wait_ge(res_done, i * RES + a + j + 1)
                ve_.tensor_scalar(den[:, j:j + 1], ps[:, j % ACCS, D:D + 1], eps, None, op).then_inc(den_done, 1)
                dve.wait_ge(den_done, i * 2 * NB + (k - 1) * NB + j + 1)
                ve_.reciprocal(rden[:, j:j + 1], den[:, j:j + 1]).then_inc(rden_done, 1)
                dve.wait_ge(rden_done, i * 3 * NB + k * NB + j + 1)

            def res2(i, j):
                divide(i, L2, j, ALU.max, DEG_EPS, 1)
                ve_.scalar_tensor_tensor(out=u[:, j % 2], in0=ps[:, j % ACCS, 0:D], scalar=rden[:, j:j + 1],
                                         in1=own[:, j], op0=ALU.mult, op1=ALU.add).then_inc(res_read, 1)
                dve.wait_ge(res_read, i * RES + L2 + j + 1)
                ve_.scalar_tensor_tensor(out=x[:, j], in0=u[:, j % 2], scalar=0.0, in1=x[:, j],
                                         op0=ALU.max, op1=ALU.add).then_inc(x2_done, 1)

            def res3a(i, j):
                divide(i, L3A, j, ALU.add, SUM_EPS, 2)
                ve_.scalar_tensor_tensor(out=g1[:, j], in0=ps[:, j % ACCS, 0:D], scalar=rden[:, j:j + 1],
                                         in1=g1[:, j], op0=ALU.mult, op1=ALU.add).then_inc(res_read, 1)

            def res3b(i, j):
                dve.wait_ge(res_done, i * RES + L3B + j + 1)
                ve_.scalar_tensor_tensor(out=u[:, j % 2], in0=ps[:, j % ACCS, 0:D], scalar=rden[:, j:j + 1],
                                         in1=own[:, j], op0=ALU.mult, op1=ALU.add).then_inc(res_read, 1)
                dve.wait_ge(res_read, i * RES + L3B + j + 1)
                ve_.scalar_tensor_tensor(out=x[:, j], in0=u[:, j % 2], scalar=0.0, in1=x[:, j],
                                         op0=ALU.max, op1=ALU.add).then_inc(out_done, 1)

            def adj_loads(i, t, layer3):
                s = t // 2 + 8 * layer3
                if t % 2 == 0:
                    dve.wait_ge(adj_loaded[s % 2], i * 128 + 16 * (s // 2 + 1))

            def product(i, t):
                c, m = divmod(t, NB)
                adj = adj_in[:, t // 2 % 2, t % 2]
                adj_loads(i, t, 0)
                ve_.tensor_copy(a_hi[:, m, chunk(c)], adj).then_inc(ahi_done, 1)
                dve.wait_ge(exp_done, i * NT + t + 1)
                ve_.tensor_tensor(p_work[:, t % RING], p_work[:, t % RING], adj, ALU.mult).then_inc(mul_done, 1)

            def p_split(i, t):
                dve.wait_ge(phi_done, i * NT + t + 1)
                ve_.tensor_tensor(p_lo[:, t % RING], p_work[:, t % RING],
                                  p_hi[:, t % RING].bitcast(F32), ALU.subtract).then_inc(plo_done, 1)

            def product3(i, t):
                c, m = divmod(t, NB)
                adj_loads(i, t, 1)
                dve.wait_ge(e3_done, i * NT + t + 1)
                ve_.tensor_tensor(a_work[:, m, chunk(c)], a_work[:, m, chunk(c)],
                                  adj_in[:, t // 2 % 2, t % 2], ALU.mult).then_inc(mul3_done, 1)

            def w_split(i, t):
                c, m = divmod(t, NB)
                dve.wait_ge(whi_done, i * NT + t + 1)
                ve_.tensor_tensor(a_lo[:, m, chunk(c)], a_work[:, m, chunk(c)],
                                  a_hi[:, m, chunk(c)].bitcast(F32), ALU.subtract).then_inc(wlo_done, 1)

            def own3(i, k):
                dve.wait_ge(g1_done, i * NB + k + 1)
                ve_.tensor_tensor(own[:, k], ps[:, S_BANK + k % 2, D:2 * D], bk_row[:], ALU.add).then_inc(own_done, 1)

            AFTER = {8: [(stats, 0), (stats, 1)], 9: [(stats, 2), (ht, 0)], 10: [(stats, 3), (ht, 1)],
                     11: [(right, 0)], 12: [(ht, 2), (right, 1)], 13: [(ht, 3), (right, 2)],
                     14: [(right, 3)]}
            with dve.Fori(0, B) as i:
                for k in range(NB + 2):
                    if k < NB:
                        stats(i, 0, k)
                    if 0 <= k - 1 < NB:
                        ht(i, 0, k - 1)
                    if k >= 2:
                        right(i, 0, k - 2)
                for v in range(4):
                    db, c = v // 2, v % 2
                    dve.wait_ge(thi_done, i * 4 + v + 1)
                    ve_.scalar_tensor_tensor(out=t_lo[:, db, chunk(c)], in0=ps[:, S_BANK + v % 2],
                                             scalar=tc[:, db:db + 1], in1=t_hi[:, db, chunk(c)].bitcast(F32),
                                             op0=ALU.add, op1=ALU.subtract).then_inc(tlo_done, 1)
                product(i, 0)
                for t in range(NT):
                    if t + 1 < NT:
                        product(i, t + 1)
                    if t == NB:
                        for j in range(BPC):
                            res0(i, j)
                    p_split(i, t)
                    for what, j in AFTER.get(t, ()):
                        what(i, 1, j)
                for j in range(BPC, NB):
                    res0(i, j)
                for l, res in ((1, None), (2, res1), (3, res2)):
                    first = BPC if l == 1 else 0
                    for k in range(first, NB + 2):
                        if k < NB:
                            if res:
                                res(i, k)
                            stats(i, l, k)
                        if first <= k - 1 < NB:
                            ht(i, l, k - 1)
                        if k - 2 >= first:
                            right(i, l, k - 2)
                own3(i, 0)
                for t in range(NT + 1):
                    if t < NT:
                        product3(i, t)
                    if t:
                        w_split(i, t - 1)
                    if t + 1 < NB:
                        own3(i, t + 1)
                    if t == 9:
                        for j in range(BPC):
                            res3a(i, j)
                for j in range(BPC, NB):
                    res3a(i, j)
                for j in range(NB):
                    res3b(i, j)

        @block.tensor
        def _(pe):
            mm = nc.tensor.matmul

            pe.wait_ge(w_loaded, 16 * N_W)
            pe.wait_ge(setup_v, SETUP_BB)
            for fb in range(FB):
                for ob in range(FB):
                    mm(ps[:, fb, 0:D], wk_raw[:, ob, blk(fb)], wq_raw[:, ob], start=ob == 0, stop=ob == 1)
                for col, (w, vec) in enumerate(((wk_raw, bq_raw), (wq_raw, bk_raw), (wv3_raw, aw_raw[:, 0]),
                                                (wv3_raw, aw_raw[:, 1]))):
                    for ob in range(FB):
                        mm(ps[:, 2 + fb, col:col + 1], w[:, ob, blk(fb)], vec[:, ob:ob + 1],
                           start=ob == 0 and col == 0, stop=ob == 1, skip_group_check=True)
            pe.wait_ge(setup_p, 3)
            for ob in range(FB):
                last = mm(ps[:, 4, 0:2], ui_full[:, 0], bb[:, :, ob], start=ob == 0, stop=ob == 1)
            last.then_inc(setup_pe, 1)
            pe.wait_ge(setup_v, SETUP_V)

            def three(out, a_hi_, a_lo_, b_hi, b_lo, first, last):
                mm(out, a_hi_, b_hi, start=first, stop=False)
                mm(out, a_hi_, b_lo, start=False, stop=False)
                return mm(out, a_lo_, b_hi, start=False, stop=last)

            def tr(i, l, j):
                q = l * NB + j
                pe.wait_ge(h_done, i * LNS + q + 1)
                if q:
                    pe.wait_ge(htlo_done, i * LNS + q)
                for fb in range(FB):
                    last = nc.tensor.transpose(ps[:, TR_BANK, blk(fb)], h[:, j % 2, blk(fb)], ident[:])
                last.then_inc(tr_done, 1)

            def pj(i, l, j):
                q = l * NB + j
                w = (wv, w1, w2, wk2)[l]
                width = w[0].shape[2]
                pe.wait_ge(htlo_done, i * LNS + q + 1)
                if q:
                    pe.wait_ge(rlo_done, i * LNS + q)
                for fb in range(FB):
                    last = three(ps[:, PJ_BANK, 0:width], ht_hi[:, fb, blk(j)], ht_lo[:, fb, blk(j)],
                                 w[0][:, fb], w[1][:, fb], fb == 0, fb == FB - 1)
                last.then_inc(pj_done, 1)

            def agg(i, a, m, j, wait=None):
                k = R_OF[a]
                n = a + j
                if m == 0 and n >= ACCS:
                    pe.wait_ge(res_read, i * RES + n - ACCS + 1)
                last = three(ps[:, j % ACCS, 0:RW], a_hi[:, m, blk(j)], a_lo[:, m, blk(j)],
                             r_hi[k][:, m], r_lo[k][:, m], m == 0, m == NB - 1)
                if m == NB - 1:
                    last.then_inc(res_done, 1)

            def group(i, a, m):
                if a == L3B:
                    pe.wait_ge(glo_done, i * NB + m + 1)
                else:
                    pe.wait_ge(rlo_done, i * LNS + a + m + 1)
                if a == L1 and m == 0:
                    pe.wait_ge(alo_done, i * NT + NT)
                for j in range(BPC):
                    agg(i, a, m, j)

            def single(i, a, j):
                for m in range(NB):
                    agg(i, a, m, j)

            def score(i, t):
                c, m = divmod(t, NB)
                if t == 0:
                    pe.wait_ge(tlo_done, i * 4 + 4)
                if t >= 2:
                    pe.wait_ge(exp_done, i * NT + t - 1)
                for db in range(FB):
                    last = three(ps[:, S_BANK + t % 2], t_hi[:, db, blk(m)], t_lo[:, db, blk(m)],
                                 ht_hi[:, db, chunk(c)], ht_lo[:, db, chunk(c)], db == 0, db == FB - 1)
                last.then_inc(s_done, 1)

            def weigh(i, t):
                c, m = divmod(t, NB)
                pe.wait_ge(plo_done, i * NT + t + 1)
                for j in range(BPC):
                    n = c * BPC + j
                    if m == 0 and n >= ACCS:
                        pe.wait_ge(res_read, i * RES + n - ACCS + 1)
                    last = three(ps[:, j, 0:RW], p_hi[:, t % RING, blk(j)], p_lo[:, t % RING, blk(j)],
                                 r_hi[0][:, m], r_lo[0][:, m], m == 0, m == NB - 1)
                    if m == NB - 1:
                        last.then_inc(res_done, 1)
                    elif j == BPC - 1:
                        last.then_inc(pv_done, 1)

            AFTER = {8: [(tr, 0)], 9: [(tr, 1)], 10: [(pj, 0)], 11: [(tr, 2), (pj, 1)],
                     12: [(tr, 3), (pj, 2)], 13: [(pj, 3)]}
            with pe.Fori(0, B) as i:
                for k in range(NB + 2):
                    if k < NB:
                        tr(i, 0, k)
                    if k >= 2:
                        pj(i, 0, k - 2)
                for v in range(4):
                    db, c = v // 2, v % 2
                    if v >= 2:
                        pe.wait_ge(tlo_done, i * 4 + v - 1)
                    for fb in range(FB):
                        last = three(ps[:, S_BANK + v % 2], wm[0][:, fb, blk(db)], wm[1][:, fb, blk(db)],
                                     ht_hi[:, fb, chunk(c)], ht_lo[:, fb, chunk(c)], fb == 0, fb == FB - 1)
                    last.then_inc(tp_done, 1)
                score(i, 0)
                score(i, 1)
                pe.wait_ge(rlo_done, i * LNS + NB)
                for t in range(NT):
                    if t + 2 < NT:
                        score(i, t + 2)
                    weigh(i, t)
                    for what, j in AFTER.get(t, ()):
                        what(i, 1, j)
                tr(i, 1, 4)
                tr(i, 1, 5)
                pj(i, 1, 4)
                group(i, L1, 0)
                tr(i, 1, 6)
                pj(i, 1, 5)
                group(i, L1, 1)
                tr(i, 1, 7)
                pj(i, 1, 6)
                group(i, L1, 2)
                pj(i, 1, 7)
                for m in range(3, NB):
                    group(i, L1, m)
                for l, a in ((2, L1), (3, L2)):
                    single(i, a, 4)
                    tr(i, l, 0)
                    tr(i, l, 1)
                    single(i, a, 5)
                    pj(i, l, 0)
                    tr(i, l, 2)
                    pj(i, l, 1)
                    tr(i, l, 3)
                    single(i, a, 6)
                    pj(i, l, 2)
                    tr(i, l, 4)
                    pj(i, l, 3)
                    single(i, a, 7)
                    tr(i, l, 5)
                    pj(i, l, 4)
                    tr(i, l, 6)
                    pj(i, l, 5)
                    if l == 2:
                        group(i, L2, 0)
                    tr(i, l, 7)
                    pj(i, l, 6)
                    if l == 2:
                        group(i, L2, 1)
                        group(i, L2, 2)
                    pj(i, l, 7)
                    if l == 2:
                        for m in range(3, NB):
                            group(i, L2, m)

                def gh(k):
                    if k == 0:
                        pe.wait_ge(si_read, i * 4 + 4)
                    if k >= 2:
                        pe.wait_ge(own_done, i * NB + k - 1)
                    for fb in range(FB):
                        last = three(ps[:, S_BANK + k % 2], ht_hi[:, fb, blk(k)], ht_lo[:, fb, blk(k)],
                                     wk10[0][:, fb], wk10[1][:, fb], fb == 0, fb == FB - 1)
                    last.then_inc(gh_done, 1)

                for c in range(2):
                    for fb in range(FB):
                        last = three(ps[:, S_BANK + c], wui[0][:, fb], wui[1][:, fb], ht_hi[:, fb, chunk(c)],
                                     ht_lo[:, fb, chunk(c)], fb == 0, fb == FB - 1)
                    last.then_inc(si_done, 1)
                gh(0)
                gh(1)
                pe.wait_ge(rlo_done, i * LNS + LNS)
                for t in range(NT):
                    if t + 2 < NB:
                        gh(t + 2)
                    c, m = divmod(t, NB)
                    pe.wait_ge(wlo_done, i * NT + t + 1)
                    for j in range(c * BPC, (c + 1) * BPC):
                        agg(i, L3A, m, j)
                for m in range(NB):
                    group(i, L3B, m)
                for j in range(BPC, NB):
                    single(i, L3B, j)


def kernel(x, adj, L0_gnn_Wq_w, L0_gnn_Wq_b, L0_gnn_Wk_w, L0_gnn_Wk_b, L0_gnn_Wv_w, L0_gnn_Wv_b,
           L1_gnn_w, L2_gnn_W, L3_gnn_Wv, L3_gnn_bv, L3_gnn_aw, L3_gnn_ab, L3_gnn_Wk, L3_gnn_bk):
    import numpy as np
    import concourse.bacc as bacc
    from concourse.bass_utils import run_bass_kernel_spmd

    def col(v):
        return np.asarray(v).reshape(-1, P).T

    def row(v):
        return np.asarray(v).reshape(1, -1)

    Wk, W2 = np.asarray(L3_gnn_Wk), np.asarray(L2_gnn_W)
    arrays = {
        "x": x,
        "adjT": np.asarray(adj).transpose(0, 2, 1),
        "wq": L0_gnn_Wq_w, "wk": L0_gnn_Wk_w,
        "bq": col(L0_gnn_Wq_b), "bk": col(L0_gnn_Wk_b),
        "wvT": np.asarray(L0_gnn_Wv_w).T, "bv": row(L0_gnn_Wv_b),
        "w1": L1_gnn_w,
        "w2": np.concatenate([W2[:, D:].T, W2[:, :D].T], axis=1),
        "wv3T": np.asarray(L3_gnn_Wv).T, "bv3": col(L3_gnn_bv),
        "aw": np.asarray(L3_gnn_aw).reshape(2, FB, P).transpose(2, 0, 1), "ab": row(L3_gnn_ab),
        "wk2": Wk[2], "wk10": np.concatenate([Wk[1], Wk[0]], axis=1),
        "bk3": L3_gnn_bk,
    }
    nc = bacc.Bacc("TRN2", target_bir_lowering=False, num_devices=1)
    arrays = {f"{n}_dram": np.ascontiguousarray(a) for n, a in arrays.items()}
    args = [nc.dram_tensor(n, a.shape, mybir.dt.from_np(a.dtype), kind="ExternalInput").ap()
            for n, a in arrays.items()]
    out = nc.dram_tensor("out_dram", (B, N, D), F32, kind="ExternalOutput").ap()
    gnn_program(nc, *args, out)
    r = run_bass_kernel_spmd(nc, [arrays], core_ids=[0])
    return r.results[0]["out_dram"]
```

```python
from contextlib import ExitStack

import concourse.bass as bass
from concourse import mybir

F32 = mybir.dt.float32
F32R = mybir.dt.float32r
ALU = mybir.AluOpType
ACT = mybir.ActivationFunctionType

P = 128
B, N, D = 8, 1024, 256
NB = N // P
FB = D // P
CH = 512
BPC = CH // P
NT = NB * (N // CH)
RW = D + 2
ACCS = 4
S_BANK = 4
HRING = 3
RING = 3
LN_EPS, DEG_EPS, SUM_EPS = 1e-5, 1e-6, 1e-12

LNS = 4 * NB
RES = 5 * NB
L0, L1, L2, L3A, L3B = (NB * k for k in range(5))


BLOCKS_PE = "O4 T0 O5 J0 T1 T2 J1 O6 T3 J2 T4 J3 O7 T5 J4 T6 J5"
BLOCKS_ACT = "N0 H0 N1 N2 R0 H1 N3 H2 R1 N4 H3 R2 N5 H4 R3 N6 H5 R4 H6 R5 N7 H7 R6 R7"
BLOCKS_DVE = ("X0 S0 X1 S1 X2 S2 H0 X3 S3 R0 H1 X4 S4 H2 R1 X5 S5 H3 X6 S6 R2 H4 R3 X7 S7 H5 R4 H6 R5 "
              "H7 R6 R7")
TAIL_PE = "E0 E1 T4 E2 T5 E3 J4 T6 J5 T7 F4 J6 F5 J7 F6 F7"
TAIL_ACT = "N4 N5 H4 N6 H5 R4 H6 N7 R5 H7 R6 R7"
TAIL_DVE = "X4 S4 X5 S5 X6 S6 X7 S7 H4 H5 R4 H6 R5 H7 R6 R7"
LAST_PE = "E0 E1 T0 E2 T1 E3 T2 F4 T3 F5 T4 F6 T5 F7 T6 O4 T7 O5 O6 O7"
LAST_DVE = "S0 S1 S2 H0 S3 H1 S4 H2 S5 H3 S6 H4 S7 H5 X0 X1 X2 X3 H6 H7 X4 X5 X6 X7"


def gnn_program(nc, x_d, adjT_d, Wq_d, Wk_d, bq_d, bk_d, WvT_d, bv_d, w1_d, w2_d,
                wv3T_d, bv3_d, aw_d, ab_d, wk2_d, wk10_d, bk3_d, out_d):
    ctx = ExitStack()
    with ctx:
        def sb(name, shape, dt=F32):
            return ctx.enter_context(nc.sbuf_tensor(name, shape, dt))

        def sem(name):
            return ctx.enter_context(nc.semaphore(name))

        KB = 1024
        base = -(-nc.sbuf_base // 32) * 32
        sb("slab", [P, 108 * KB // 4])

        def at(name, shape, dt, off):
            return nc.alloc_sbuf_tensor_at(name, shape, dt, offset=base + off)

        a_hi = at("a_hi", [P, NB, N], F32R, 0)
        a_lo = at("a_lo", [P, NB, N], F32R, 32 * KB)
        a_work = at("a_work", [P, NB, N], F32, 32 * KB)
        t_hi = at("t_hi", [P, FB, N], F32R, 64 * KB)
        t_lo = at("t_lo", [P, FB, N], F32R, 72 * KB)
        g1 = at("g1", [P, NB, D], F32, 64 * KB)
        si = at("si", [P, N], F32, 72 * KB)
        si2 = at("si2", [P, N], F32, 76 * KB)
        p_hi = at("p_hi", [P, RING, CH], F32R, 80 * KB)
        p_lo = at("p_lo", [P, RING, CH], F32R, 86 * KB)
        p_work = at("p_work", [P, RING, CH], F32, 86 * KB)
        own = at("own", [P, NB, D], F32, 80 * KB)
        ht_hi = at("ht_hi", [P, FB, N], F32R, 92 * KB)
        ht_lo = at("ht_lo", [P, FB, N], F32R, 100 * KB)
        wq_raw = at("wq_raw", [P, FB, D], F32, 0)
        wk_raw = at("wk_raw", [P, FB, D], F32, 2 * KB)
        wv_raw = at("wv_raw", [P, FB, D], F32, 4 * KB)
        w1_raw = at("w1_raw", [P, FB, D], F32, 6 * KB)
        wv3_raw = at("wv3_raw", [P, FB, D], F32, 8 * KB)
        wk2_raw = at("wk2_raw", [P, FB, D], F32, 10 * KB)
        w2_raw = at("w2_raw", [P, FB, 2 * D], F32, 12 * KB)
        wk10_raw = at("wk10_raw", [P, FB, 2 * D], F32, 16 * KB)
        bk3_raw = at("bk3_raw", [P, 3, D], F32, 20 * KB)
        bq_raw = at("bq_raw", [P, FB], F32, 23 * KB)
        bk_raw = at("bk_raw", [P, FB], F32, 23 * KB + 32)
        bv3_raw = at("bv3_raw", [P, FB], F32, 23 * KB + 64)
        aw_raw = at("aw_raw", [P, 2, FB], F32, 23 * KB + 96)
        ab_raw = at("ab_raw", [P, 1], F32, 23 * KB + 128)
        bb = at("bb", [P, 2, FB], F32, 23 * KB + 160)
        aws = at("aws", [P, FB], F32, 23 * KB + 192)
        urow = at("urow", [P, FB, 4], F32, 23 * KB + 224)
        ui_full = at("ui_full", [P, FB, P], F32, 24 * KB)
        sums = at("sums", [P, 2], F32, 25 * KB)
        bk_two = at("bk_two", [P, D], F32, 26 * KB)

        x_in = sb("x_in", [P, NB, D])
        x = sb("x", [P, NB, D])
        r_hi = [sb(f"r{k}_hi", [P, NB, RW], F32R) for k in range(2)]
        r_lo = [sb(f"r{k}_lo", [P, NB, RW], F32R) for k in range(2)]
        adj_in = sb("adj_in", [P, 2, 2, CH])
        wm = [sb(f"wm_{s}", [P, FB, D], F32R) for s in ("hi", "lo")]
        wv = [sb(f"wv_{s}", [P, FB, RW], F32R) for s in ("hi", "lo")]
        w1 = [sb(f"w1_{s}", [P, FB, D], F32R) for s in ("hi", "lo")]
        w2 = [sb(f"w2_{s}", [P, FB, 2 * D], F32R) for s in ("hi", "lo")]
        wk2 = [sb(f"wk2_{s}", [P, FB, RW], F32R) for s in ("hi", "lo")]
        wk10 = [sb(f"wk10_{s}", [P, FB, 2 * D], F32R) for s in ("hi", "lo")]
        wui = [sb(f"wui_{s}", [P, FB, P], F32R) for s in ("hi", "lo")]
        bv_row = sb("bv_row", [P, D])
        bk_row = sb("bk_row", [P, D])
        h = sb("h", [P, HRING, D])
        u = sb("u", [P, 2, D])
        ident = sb("ident", [P, P])
        bn = sb("bn", [P, NB, 6])
        mv = sb("mv", [P, NB, 2])
        ve = sb("ve", [P, NB])
        rstd = sb("rstd", [P, NB])
        nmr = sb("nmr", [P, NB])
        minus_half = sb("minus_half", [P, 1])
        tc = sb("tc", [P, FB])
        g0 = sb("g0", [P, 1])
        s0 = sb("s0", [P, 1])
        g = sb("g", [P, NB])
        sj8 = sb("sj8", [P, NB])
        sj2 = sb("sj2", [P, NB])
        den = sb("den", [P, NB])
        rden = sb("rden", [P, NB])
        ps = ctx.enter_context(nc.psum_tensor("ps", [P, 8, CH], F32))

        passed_sp, passed_v, passed_p = sem("passed_sp"), sem("passed_v"), sem("passed_p")
        w_loaded, x_loaded, stored = sem("w_loaded"), sem("x_loaded"), sem("stored")
        adj_loaded = [sem("adj_loaded0"), sem("adj_loaded1")]
        setup_v, setup_p, setup_pe = sem("setup_v"), sem("setup_p"), sem("setup_pe")
        bn_done, mv_done = sem("bn_done"), sem("mv_done")
        ve_done, rstd_done, nmr_done = sem("ve_done"), sem("rstd_done"), sem("nmr_done")
        xb_done = sem("xb_done")
        h_done, hthi_done = sem("h_done"), sem("hthi_done")
        tr_done = sem("tr_done")
        htlo_done = sem("htlo_done")
        pj_done, rhi_done, rlo_done = sem("pj_done"), sem("rhi_done"), sem("rlo_done")
        tp_done, thi_done, tlo_done = sem("tp_done"), sem("thi_done"), sem("tlo_done")
        s_done, exp_done, mul_done = sem("s_done"), sem("exp_done"), sem("mul_done")
        phi_done, plo_done, pv_done = sem("phi_done"), sem("plo_done"), sem("pv_done")
        ahi_done, alo_done = sem("ahi_done"), sem("alo_done")
        res_done, res_read = sem("res_done"), sem("res_read")
        den_done, rden_done, x2_done, out_done = sem("den_done"), sem("rden_done"), sem("x2_done"), sem("out_done")
        si_done, si_read = sem("si_done"), sem("si_read")
        relu_done, add_done, e3_done = sem("relu_done"), sem("add_done"), sem("e3_done")
        mul3_done, whi_done, wlo_done = sem("mul3_done"), sem("whi_done"), sem("wlo_done")
        gh_done, g1_done, own_done = sem("gh_done"), sem("g1_done"), sem("own_done")
        ghi_done, glo_done = sem("ghi_done"), sem("glo_done")

        SETUP_BB = 2 + 2 + 1 + 2 * 5 + 5 + 2
        SETUP_V = SETUP_BB + FB * (2 * 3 + 3 + 2) + 4
        R_OF = {L0: 0, L1: 1, L2: 0, L3A: 1, L3B: 0}
        N_W = 15

        def tr_bank(l, j):
            return 7 if j % 2 == 0 or (l == 1 and j < BPC) else 5

        def pj_bank(l, j):
            return 6 if j % 2 == 0 or (l == 1 and j < BPC) else 4

        def last_use(bank, l, j):
            q = l * NB + j
            return next((p + 1 for p in range(q - 1, -1, -1) if bank(*divmod(p, NB)) == bank(l, j)), 0)

        T_BANKS = (7, 5, 6, 4)
        SI_BANKS = (7, 5)
        GH_BANKS = (6, 4)
        NEXT = 4

        def blk(j):
            return slice(j * P, (j + 1) * P)

        def chunk(c):
            return slice(c * CH, (c + 1) * CH)

        block = ctx.enter_context(nc.Block())

        @block.sync
        def _(sp):
            def halves(w):
                return w.rearrange("(a p) n -> p a n", p=P)
            for dst, src in (
                (wq_raw[:], halves(Wq_d)), (wk_raw[:], halves(Wk_d)), (wv_raw[:], halves(WvT_d)),
                (w1_raw[:], halves(w1_d)), (wv3_raw[:], halves(wv3T_d)), (wk2_raw[:], halves(wk2_d)),
                (w2_raw[:], halves(w2_d)), (wk10_raw[:], halves(wk10_d)),
                (bk3_raw[:], bk3_d.partition_broadcast(P)), (bv_row[:], bv_d.partition_broadcast(P)),
                (bq_raw[:], bq_d), (bk_raw[:], bk_d), (bv3_raw[:], bv3_d), (aw_raw[:], aw_d),
                (ab_raw[:], ab_d.partition_broadcast(P)),
            ):
                sp.dma_start(dst, src).then_inc(w_loaded, 16)

            def load_x(i):
                sp.dma_start(x_in[:], x_d[bass.ds(i, 1)].rearrange("b (j p) d -> p (b j) d", p=P)
                             if not isinstance(i, int) else
                             x_d[i].rearrange("(j p) d -> p j d", p=P)).then_inc(x_loaded, 16)

            def load_adj(i, s):
                c, pair = s % 8 // 4, s % 4
                src = adjT_d[i] if isinstance(i, int) else adjT_d[bass.ds(i, 1)]
                if isinstance(i, int):
                    src = src.rearrange("(a m p) n -> a p m n", m=2, p=P)[pair][:, :, chunk(c)]
                else:
                    src = src.rearrange("b (a m p) n -> a p (b m) n", m=2, p=P)[pair][:, :, chunk(c)]
                sp.dma_start(adj_in[:, s % 2], src).then_inc(adj_loaded[s % 2], 16)

            def freed(i, s):
                if s <= 9:
                    sp.wait_ge(mul_done, i * NT + 2 * (s - 1))
                    sp.wait_ge(alo_done, i * NT + 2 * (s - 1))
                else:
                    sp.wait_ge(mul3_done, i * NT + 2 * (s - 9))
                sp.sem_inc(passed_sp, 1)

            def graph(i, more):
                for s in range(2, 8):
                    freed(i, s)
                    load_adj(i, s)
                sp.wait_ge(res_read, i * RES + L1)
                sp.sem_inc(passed_sp, 1)
                load_x(i + 1 if more else i)
                for s in range(8, 16):
                    freed(i, s)
                    load_adj(i, s)
                if more:
                    for s in range(16, 18):
                        freed(i, s)
                        load_adj(i + 1, s - 16)

            load_x(0)
            for s in range(2):
                load_adj(0, s)
            with sp.Fori(0, B - 1) as i:
                graph(i, True)
            graph(B - 1, False)

        @block.gpsimd
        def _(pool):
            gp = nc.gpsimd
            gp.memset(ident[:], 0.0).then_inc(setup_p, 1)
            gp.memset(minus_half[:], -0.5).then_inc(setup_p, 1)
            pool.wait_ge(setup_p, 2)
            gp.affine_select(out=ident[:], in_=ident[:], compare_op=ALU.not_equal, fill=1.0, base=0,
                             pattern=[[-1, P]], channel_multiplier=1).then_inc(setup_p, 1)
            pool.wait_ge(w_loaded, 16 * N_W)

            def rstds(i, l, j):
                q = l * NB + j + 1
                pool.wait_ge(mv_done, i * LNS + q)
                pool.sem_inc(passed_p, 1)
                gp.tensor_scalar(ve[:, j:j + 1], mv[:, j, 1:2], LN_EPS, 1.0, ALU.add, ALU.mult).then_inc(ve_done, 1)
                pool.wait_ge(ve_done, i * LNS + q)
                gp.tensor_tensor(rstd[:, j:j + 1], ve[:, j:j + 1], minus_half[:], ALU.pow).then_inc(rstd_done, 1)
                pool.wait_ge(rstd_done, i * LNS + q)
                pool.sem_inc(passed_p, 1)
                gp.tensor_scalar(nmr[:, j:j + 1], mv[:, j, 0:1], rstd[:, j:j + 1], -1.0,
                                 ALU.mult, ALU.mult).then_inc(nmr_done, 1)

            def split_adj(i, t):
                c, m = divmod(t, NB)
                pool.wait_ge(ahi_done, i * NT + t + 1)
                gp.tensor_tensor(a_lo[:, m, chunk(c)], adj_in[:, t // 2 % 2, t % 2],
                                 a_hi[:, m, chunk(c)].bitcast(F32), ALU.subtract).then_inc(alo_done, 1)

            def add3(i, t):
                c, m = divmod(t, NB)
                pool.wait_ge(relu_done, i * NT + t + 1)
                gp.tensor_tensor(a_work[:, m, chunk(c)], a_work[:, m, chunk(c)], si2[:, chunk(c)],
                                 ALU.add).then_inc(add_done, 1)

            def split_g(i, j):
                pool.wait_ge(ghi_done, i * NB + j + 1)
                gp.tensor_tensor(r_lo[0][:, j, 0:D], g1[:, j], r_hi[0][:, j, 0:D].bitcast(F32),
                                 ALU.subtract).then_inc(glo_done, 1)

            for j in range(NB):
                rstds(0, 0, j)
            with pool.Fori(0, B) as i:
                for j in range(NB):
                    pool.wait_ge(h_done, i * LNS + j + 1)
                    gp.tensor_tensor(x_in[:, j], x_in[:, j], bv_row[:], ALU.add).then_inc(xb_done, 1)
                for t in range(NT):
                    split_adj(i, t)
                    if t in (8, 9, 10, 11):
                        rstds(i, 1, t - 8)
                for j in range(BPC, NB):
                    rstds(i, 1, j)
                for l in (2, 3):
                    for j in range(NB):
                        rstds(i, l, j)
                for t in range(NT):
                    add3(i, t)
                    if t == 13:
                        for j in range(BPC):
                            split_g(i, j)
                for j in range(BPC, NB):
                    split_g(i, j)
                for j in range(NB):
                    rstds(i, NEXT, j)

        @block.scalar
        def _(act):
            sc = nc.scalar

            def norm(i, l, j):
                q = l * NB + j + 1
                act.wait_ge(nmr_done, i * LNS + q)
                if q > HRING:
                    act.wait_ge(tr_done, i * LNS + q - HRING)
                src = x_in if l in (0, NEXT) else x
                sc.activation(h[:, (q - 1) % HRING], src[:, j], ACT.Relu, bias=nmr[:, j:j + 1],
                              scale=rstd[:, j:j + 1]).then_inc(h_done, 1)

            def ht(i, l, j):
                act.wait_ge(tr_done, i * LNS + l * NB + j + 1)
                sc.copy(ht_hi[:, :, blk(j)],
                        ps[:, tr_bank(l, j), 0:D].rearrange("p (a n) -> p a n", a=FB)).then_inc(hthi_done, 1)

            def right(i, l, j):
                k = l % 2
                act.wait_ge(pj_done, i * LNS + l * NB + j + 1)
                if l == 2:
                    sc.copy(own[:, j], ps[:, pj_bank(l, j), D:2 * D])
                sc.copy(r_hi[k][:, j, 0:D], ps[:, pj_bank(l, j), 0:D]).then_inc(rhi_done, 1)

            def t_split(i, v):
                db, c = v // 2, v % 2
                act.wait_ge(tp_done, i * 4 + v + 1)
                sc.activation(t_hi[:, db, chunk(c)], ps[:, T_BANKS[v]], ACT.Identity,
                              bias=tc[:, db:db + 1]).then_inc(thi_done, 1)

            def weighed(i, t):
                c, m = divmod(t, NB)
                if m == NB - 1:
                    act.wait_ge(res_done, i * RES + (c + 1) * BPC)
                else:
                    act.wait_ge(pv_done, i * (NT - 2) + t - c + 1)

            def expo(i, t):
                m = t % NB
                act.wait_ge(s_done, i * NT + t + 1)
                if t >= RING:
                    weighed(i, t - RING)
                sc.activation(p_work[:, t % RING], ps[:, S_BANK + t % 2], ACT.Exp,
                              bias=g[:, m:m + 1]).then_inc(exp_done, 1)

            def p_split(i, t):
                act.wait_ge(mul_done, i * NT + t + 1)
                sc.copy(p_hi[:, t % RING], p_work[:, t % RING]).then_inc(phi_done, 1)

            def relu3(i, t):
                c, m = divmod(t, NB)
                if t == 0:
                    act.wait_ge(rlo_done, i * LNS + LNS)
                    act.wait_ge(si_read, i * 4 + 4)
                sc.activation(a_work[:, m, chunk(c)], si[:, chunk(c)], ACT.Relu, scale=0.8,
                              bias=sj8[:, m:m + 1]).then_inc(relu_done, 1)

            def exp3(i, t):
                c, m = divmod(t, NB)
                act.wait_ge(add_done, i * NT + t + 1)
                sc.activation(a_work[:, m, chunk(c)], a_work[:, m, chunk(c)], ACT.Exp,
                              bias=sj2[:, m:m + 1]).then_inc(e3_done, 1)

            def w_split(i, t):
                c, m = divmod(t, NB)
                act.wait_ge(mul3_done, i * NT + t + 1)
                sc.copy(a_hi[:, m, chunk(c)], a_work[:, m, chunk(c)]).then_inc(whi_done, 1)

            def g1_copy(i, k):
                act.wait_ge(gh_done, i * NB + k + 1)
                sc.copy(g1[:, k], ps[:, GH_BANKS[k % 2], 0:D]).then_inc(g1_done, 1)

            def g_split(i, j):
                act.wait_ge(res_read, i * RES + L3A + j + 1)
                sc.copy(r_hi[0][:, j, 0:D], g1[:, j]).then_inc(ghi_done, 1)

            act.wait_ge(setup_v, SETUP_V)
            AFTER = {8: [(norm, 0), (norm, 1)], 9: [(ht, 0)], 10: [(norm, 2), (ht, 1)],
                     11: [(norm, 3), (right, 0)], 12: [(ht, 2), (right, 1)],
                     13: [(ht, 3), (right, 2)], 14: [(right, 3)]}
            steps = {"N": norm, "H": ht, "R": right}
            for j in range(NB):
                norm(0, 0, j)
                ht(0, 0, j)
            with act.Fori(0, B) as i:
                for j in range(NB):
                    right(i, 0, j)
                for v in range(4):
                    t_split(i, v)
                expo(i, 0)
                for t in range(NT):
                    if t + 1 < NT:
                        expo(i, t + 1)
                    p_split(i, t)
                    for what, j in AFTER.get(t, ()):
                        what(i, 1, j)
                for l, order in ((1, TAIL_ACT), (2, BLOCKS_ACT), (3, BLOCKS_ACT)):
                    for what, j in order.split():
                        steps[what](i, l, int(j))
                for c in range(2):
                    act.wait_ge(si_done, i * 2 + c + 1)
                    sc.copy(si[:, chunk(c)], ps[:, SI_BANKS[c]]).then_inc(si_read, 1)
                    sc.mul(si2[:, chunk(c)], ps[:, SI_BANKS[c]], 0.2).then_inc(si_read, 1)
                for t in range(3):
                    relu3(i, t)
                g1_copy(i, 0)
                for t in range(NT + 1):
                    if t < NT:
                        exp3(i, t)
                    if t:
                        w_split(i, t - 1)
                    if t + 3 < NT:
                        relu3(i, t + 3)
                    if t + 1 < NB:
                        g1_copy(i, t + 1)
                    if t == 10:
                        for j in range(BPC):
                            g_split(i, j)
                for j in range(BPC, NB):
                    g_split(i, j)
                for j in range(NB):
                    norm(i, NEXT, j)
                    ht(i, NEXT, j)
                for c in range(2):
                    act.wait_ge(out_done, i * NB + (c + 1) * BPC)
                    act.dma_start(out_d[bass.ds(i, 1)].rearrange("b (c j p) d -> c p (b j) d", c=2, p=P)[c],
                                  x[:, c * BPC:(c + 1) * BPC]).then_inc(stored, 16)
            act.wait_ge(stored, 16 + 32 * B)

        @block.vector
        def _(dve):
            ve_ = nc.vector
            steps = [0]

            def link(ins):
                steps[0] += 1
                ins.then_inc(setup_v, 1)
                dve.wait_ge(setup_v, steps[0])

            def split(pair, dst, src):
                link(ve_.tensor_copy(dst(pair[0]), src))
                link(ve_.tensor_tensor(dst(pair[1]), src, dst(pair[0]).bitcast(F32), ALU.subtract))

            for k in range(2):
                ve_.memset(r_hi[k][:, :, D:D + 1].bitcast(F32), 1.0)
                ve_.memset(r_hi[k][:, :, D + 1:RW].bitcast(F32), 0.0)
                link(ve_.memset(r_lo[k][:, :, D:RW].bitcast(F32), 0.0))
            for w in wv + wk2:
                link(ve_.memset(w[:, :, D:RW].bitcast(F32), 0.0))
            link(ve_.memset(ui_full[:], 1.0))
            dve.wait_ge(w_loaded, 16 * N_W)
            for pair, raw in ((wv, wv_raw), (w1, w1_raw), (wk2, wk2_raw)):
                split(pair, lambda w: w[:, :, 0:D], raw[:])
            for pair, raw in ((w2, w2_raw), (wk10, wk10_raw)):
                split(pair, lambda w: w[:], raw[:])
            link(ve_.tensor_tensor(bk_two[:], bk3_raw[:, 0], bk3_raw[:, 1], ALU.add))
            link(ve_.tensor_tensor(bk_row[:], bk_two[:], bk3_raw[:, 2], ALU.add))
            link(ve_.tensor_tensor(bb[:, 0], bq_raw[:], bk_raw[:], ALU.mult))
            link(ve_.tensor_tensor(aws[:], aw_raw[:, 0], aw_raw[:, 1], ALU.add))
            link(ve_.tensor_tensor(bb[:, 1], bv3_raw[:], aws[:], ALU.mult))
            assert steps[0] == SETUP_BB
            dve.wait_ge(setup_pe, 1)
            for fb in range(FB):
                split(wm, lambda w: w[:, fb], ps[:, fb, 0:D])
                split(wv, lambda w: w[:, fb, D:D + 1], ps[:, 2 + fb, 0:1])
                split(wk2, lambda w: w[:, fb, D:D + 1], ps[:, 2 + fb, 2:3])
                link(ve_.tensor_copy(tc[:, fb:fb + 1], ps[:, 2 + fb, 1:2]))
                link(ve_.tensor_copy(urow[:, fb, 0:1], ps[:, 2 + fb, 3:4]))
                link(ve_.tensor_scalar(ui_full[:, fb], ui_full[:, fb], urow[:, fb, 0:1], None, ALU.mult))
                split(wui, lambda w: w[:, fb], ui_full[:, fb])
            link(ve_.tensor_copy(sums[:, 0:1], ps[:, 4, 0:1]))
            link(ve_.tensor_copy(sums[:, 1:2], ps[:, 4, 1:2]))
            link(ve_.tensor_copy(g0[:], sums[:, 0:1]))
            link(ve_.tensor_tensor(s0[:], sums[:, 1:2], ab_raw[:], ALU.add))
            ve_.memset(u[:, 0, 0:1], 0.0).then_inc(stored, 16)
            assert steps[0] == SETUP_V, steps[0]

            def stats(i, l, j):
                q = l * NB + j + 1
                if l in (0, NEXT):
                    if j == 0:
                        dve.wait_ge(x_loaded, i * 16 + (16 if l == 0 else 32))
                elif l == 3:
                    dve.wait_ge(x2_done, i * NB + j + 1)
                else:
                    dve.wait_ge(res_read, i * RES + (l - 1) * NB + j + 1)
                src = x_in if l in (0, NEXT) else x
                ve_.bn_stats(bn[:, j], src[:, j]).then_inc(bn_done, 1)
                dve.wait_ge(bn_done, i * LNS + q)
                dve.sem_inc(passed_v, 1)
                ve_.bn_aggr(mv[:, j], bn[:, j]).then_inc(mv_done, 1)

            def ht(i, l, j):
                dve.wait_ge(hthi_done, i * LNS + l * NB + j + 1)
                ve_.tensor_tensor(ht_lo[:, :, blk(j)], ps[:, tr_bank(l, j), 0:D].rearrange("p (a n) -> p a n", a=FB),
                                  ht_hi[:, :, blk(j)].bitcast(F32), ALU.subtract).then_inc(htlo_done, 1)

            def right(i, l, j):
                k = l % 2
                dve.wait_ge(rhi_done, i * LNS + l * NB + j + 1)
                last = ps[:, pj_bank(l, j), D:D + 1]
                if l == 0:
                    ve_.tensor_scalar(g[:, j:j + 1], last, g0[:], None, ALU.add)
                if l == 3:
                    ve_.tensor_scalar(sj8[:, j:j + 1], last, s0[:], 0.8, ALU.add, ALU.mult)
                    ve_.tensor_scalar(sj2[:, j:j + 1], last, s0[:], 0.2, ALU.add, ALU.mult)
                ve_.tensor_tensor(r_lo[k][:, j, 0:D], ps[:, pj_bank(l, j), 0:D],
                                  r_hi[k][:, j, 0:D].bitcast(F32), ALU.subtract).then_inc(rlo_done, 1)

            def res0(i, j):
                dve.wait_ge(res_done, i * RES + L0 + j + 1)
                ve_.reciprocal(rden[:, j:j + 1], ps[:, j % ACCS, D:D + 1]).then_inc(rden_done, 1)
                if j == 0:
                    dve.wait_ge(stored, i * 32 + 16)
                dve.wait_ge(xb_done, i * NB + j + 1)
                dve.wait_ge(rden_done, i * 3 * NB + j + 1)
                ve_.scalar_tensor_tensor(out=x[:, j], in0=ps[:, j % ACCS, 0:D], scalar=rden[:, j:j + 1],
                                         in1=x_in[:, j], op0=ALU.mult, op1=ALU.add).then_inc(res_read, 1)

            def res1(i, j):
                dve.wait_ge(res_done, i * RES + L1 + j + 1)
                ve_.tensor_tensor(x[:, j], ps[:, j % ACCS, 0:D], x[:, j], ALU.add).then_inc(res_read, 1)

            def divide(i, a, j, op, eps, k):
                dve.wait_ge(res_done, i * RES + a + j + 1)
                ve_.tensor_scalar(den[:, j:j + 1], ps[:, j % ACCS, D:D + 1], eps, None, op).then_inc(den_done, 1)
                dve.wait_ge(den_done, i * 2 * NB + (k - 1) * NB + j + 1)
                ve_.reciprocal(rden[:, j:j + 1], den[:, j:j + 1]).then_inc(rden_done, 1)
                dve.wait_ge(rden_done, i * 3 * NB + k * NB + j + 1)

            def res2(i, j):
                divide(i, L2, j, ALU.max, DEG_EPS, 1)
                ve_.scalar_tensor_tensor(out=u[:, j % 2], in0=ps[:, j % ACCS, 0:D], scalar=rden[:, j:j + 1],
                                         in1=own[:, j], op0=ALU.mult, op1=ALU.add).then_inc(res_read, 1)
                dve.wait_ge(res_read, i * RES + L2 + j + 1)
                ve_.scalar_tensor_tensor(out=x[:, j], in0=u[:, j % 2], scalar=0.0, in1=x[:, j],
                                         op0=ALU.max, op1=ALU.add).then_inc(x2_done, 1)

            def res3a(i, j):
                divide(i, L3A, j, ALU.add, SUM_EPS, 2)
                ve_.scalar_tensor_tensor(out=g1[:, j], in0=ps[:, j % ACCS, 0:D], scalar=rden[:, j:j + 1],
                                         in1=g1[:, j], op0=ALU.mult, op1=ALU.add).then_inc(res_read, 1)

            def res3b(i, j):
                dve.wait_ge(res_done, i * RES + L3B + j + 1)
                ve_.scalar_tensor_tensor(out=u[:, j % 2], in0=ps[:, j % ACCS, 0:D], scalar=rden[:, j:j + 1],
                                         in1=own[:, j], op0=ALU.mult, op1=ALU.add).then_inc(res_read, 1)
                dve.wait_ge(res_read, i * RES + L3B + j + 1)
                ve_.scalar_tensor_tensor(out=x[:, j], in0=u[:, j % 2], scalar=0.0, in1=x[:, j],
                                         op0=ALU.max, op1=ALU.add).then_inc(out_done, 1)

            def adj_loads(i, t, layer3):
                s = t // 2 + 8 * layer3
                if t % 2 == 0:
                    dve.wait_ge(adj_loaded[s % 2], i * 128 + 16 * (s // 2 + 1))

            def product(i, t):
                c, m = divmod(t, NB)
                adj = adj_in[:, t // 2 % 2, t % 2]
                adj_loads(i, t, 0)
                ve_.tensor_copy(a_hi[:, m, chunk(c)], adj).then_inc(ahi_done, 1)
                dve.wait_ge(exp_done, i * NT + t + 1)
                ve_.tensor_tensor(p_work[:, t % RING], p_work[:, t % RING], adj, ALU.mult).then_inc(mul_done, 1)

            def p_split(i, t):
                dve.wait_ge(phi_done, i * NT + t + 1)
                ve_.tensor_tensor(p_lo[:, t % RING], p_work[:, t % RING],
                                  p_hi[:, t % RING].bitcast(F32), ALU.subtract).then_inc(plo_done, 1)

            def product3(i, t):
                c, m = divmod(t, NB)
                adj_loads(i, t, 1)
                dve.wait_ge(e3_done, i * NT + t + 1)
                ve_.tensor_tensor(a_work[:, m, chunk(c)], a_work[:, m, chunk(c)],
                                  adj_in[:, t // 2 % 2, t % 2], ALU.mult).then_inc(mul3_done, 1)

            def w_split(i, t):
                c, m = divmod(t, NB)
                dve.wait_ge(whi_done, i * NT + t + 1)
                ve_.tensor_tensor(a_lo[:, m, chunk(c)], a_work[:, m, chunk(c)],
                                  a_hi[:, m, chunk(c)].bitcast(F32), ALU.subtract).then_inc(wlo_done, 1)

            def own3(i, k):
                dve.wait_ge(g1_done, i * NB + k + 1)
                ve_.tensor_tensor(own[:, k], ps[:, GH_BANKS[k % 2], D:2 * D], bk_row[:], ALU.add).then_inc(own_done, 1)

            AFTER = {8: [(stats, 0), (stats, 1)], 9: [(stats, 2), (ht, 0)], 10: [(stats, 3), (ht, 1)],
                     11: [(right, 0)], 12: [(ht, 2), (right, 1)], 13: [(ht, 3), (right, 2)],
                     14: [(right, 3)]}
            for j in range(NB):
                stats(0, 0, j)
                if j >= 2:
                    ht(0, 0, j - 2)
            ht(0, 0, NB - 2)
            ht(0, 0, NB - 1)
            with dve.Fori(0, B) as i:
                for j in range(NB):
                    right(i, 0, j)
                for v in range(4):
                    db, c = v // 2, v % 2
                    dve.wait_ge(thi_done, i * 4 + v + 1)
                    ve_.scalar_tensor_tensor(out=t_lo[:, db, chunk(c)], in0=ps[:, T_BANKS[v]],
                                             scalar=tc[:, db:db + 1], in1=t_hi[:, db, chunk(c)].bitcast(F32),
                                             op0=ALU.add, op1=ALU.subtract).then_inc(tlo_done, 1)
                product(i, 0)
                for t in range(NT):
                    if t + 1 < NT:
                        product(i, t + 1)
                    if t == NB:
                        for j in range(BPC):
                            res0(i, j)
                    p_split(i, t)
                    for what, j in AFTER.get(t, ()):
                        what(i, 1, j)
                for l, res, order in ((1, res0, TAIL_DVE), (2, res1, BLOCKS_DVE), (3, res2, BLOCKS_DVE)):
                    steps = {"X": res, "S": lambda i, j: stats(i, l, j), "H": lambda i, j: ht(i, l, j),
                             "R": lambda i, j: right(i, l, j)}
                    for what, j in order.split():
                        steps[what](i, int(j))
                own3(i, 0)
                for t in range(NT + 1):
                    if t < NT:
                        product3(i, t)
                    if t:
                        w_split(i, t - 1)
                    if t + 1 < NB:
                        own3(i, t + 1)
                    if t == 9:
                        for j in range(BPC):
                            res3a(i, j)
                for j in range(BPC, NB):
                    res3a(i, j)
                for what, j in LAST_DVE.split():
                    {"X": res3b, "S": lambda i, j: stats(i, NEXT, j),
                     "H": lambda i, j: ht(i, NEXT, j)}[what](i, int(j))

        @block.tensor
        def _(pe):
            mm = nc.tensor.matmul

            pe.wait_ge(w_loaded, 16 * N_W)
            pe.wait_ge(setup_v, SETUP_BB)
            for fb in range(FB):
                for ob in range(FB):
                    mm(ps[:, fb, 0:D], wk_raw[:, ob, blk(fb)], wq_raw[:, ob], start=ob == 0, stop=ob == 1)
                for col, (w, vec) in enumerate(((wk_raw, bq_raw), (wq_raw, bk_raw), (wv3_raw, aw_raw[:, 0]),
                                                (wv3_raw, aw_raw[:, 1]))):
                    for ob in range(FB):
                        mm(ps[:, 2 + fb, col:col + 1], w[:, ob, blk(fb)], vec[:, ob:ob + 1],
                           start=ob == 0 and col == 0, stop=ob == 1, skip_group_check=True)
            pe.wait_ge(setup_p, 3)
            for ob in range(FB):
                last = mm(ps[:, 4, 0:2], ui_full[:, 0], bb[:, :, ob], start=ob == 0, stop=ob == 1)
            last.then_inc(setup_pe, 1)
            pe.wait_ge(setup_v, SETUP_V)

            def three(out, a_hi_, a_lo_, b_hi, b_lo, first, last):
                mm(out, a_hi_, b_hi, start=first, stop=False)
                mm(out, a_hi_, b_lo, start=False, stop=False)
                return mm(out, a_lo_, b_hi, start=False, stop=last)

            def tr(i, l, j):
                q = l * NB + j
                pe.wait_ge(h_done, i * LNS + q + 1)
                if last_use(tr_bank, l, j):
                    pe.wait_ge(htlo_done, i * LNS + last_use(tr_bank, l, j))
                for fb in range(FB):
                    last = nc.tensor.transpose(ps[:, tr_bank(l, j), blk(fb)], h[:, q % HRING, blk(fb)], ident[:])
                last.then_inc(tr_done, 1)

            def pj(i, l, j):
                q = l * NB + j
                w = (wv, w1, w2, wk2)[l]
                width = w[0].shape[2]
                pe.wait_ge(htlo_done, i * LNS + q + 1)
                if last_use(pj_bank, l, j):
                    pe.wait_ge(rlo_done, i * LNS + last_use(pj_bank, l, j))
                for fb in range(FB):
                    last = three(ps[:, pj_bank(l, j), 0:width], ht_hi[:, fb, blk(j)], ht_lo[:, fb, blk(j)],
                                 w[0][:, fb], w[1][:, fb], fb == 0, fb == FB - 1)
                last.then_inc(pj_done, 1)

            def agg(i, a, m, j, wait=None):
                k = R_OF[a]
                n = a + j
                if m == 0 and n >= ACCS:
                    pe.wait_ge(res_read, i * RES + n - ACCS + 1)
                last = three(ps[:, j % ACCS, 0:RW], a_hi[:, m, blk(j)], a_lo[:, m, blk(j)],
                             r_hi[k][:, m], r_lo[k][:, m], m == 0, m == NB - 1)
                if m == NB - 1:
                    last.then_inc(res_done, 1)

            def group(i, a, m):
                if a == L3B:
                    pe.wait_ge(glo_done, i * NB + m + 1)
                else:
                    pe.wait_ge(rlo_done, i * LNS + a + m + 1)
                for j in range(BPC):
                    agg(i, a, m, j)

            def single(i, a, j):
                for m in range(NB):
                    agg(i, a, m, j)

            def score(i, t):
                c, m = divmod(t, NB)
                if t == 0:
                    pe.wait_ge(tlo_done, i * 4 + 4)
                if t >= 2:
                    pe.wait_ge(exp_done, i * NT + t - 1)
                for db in range(FB):
                    last = three(ps[:, S_BANK + t % 2], t_hi[:, db, blk(m)], t_lo[:, db, blk(m)],
                                 ht_hi[:, db, chunk(c)], ht_lo[:, db, chunk(c)], db == 0, db == FB - 1)
                last.then_inc(s_done, 1)

            def weigh(i, t):
                c, m = divmod(t, NB)
                pe.wait_ge(plo_done, i * NT + t + 1)
                for j in range(BPC):
                    n = c * BPC + j
                    if m == 0 and n >= ACCS:
                        pe.wait_ge(res_read, i * RES + n - ACCS + 1)
                    last = three(ps[:, j, 0:RW], p_hi[:, t % RING, blk(j)], p_lo[:, t % RING, blk(j)],
                                 r_hi[0][:, m], r_lo[0][:, m], m == 0, m == NB - 1)
                    if m == NB - 1:
                        last.then_inc(res_done, 1)
                    elif j == BPC - 1:
                        last.then_inc(pv_done, 1)

            def run(i, l, a, order):
                f = {L0: L1, L1: L2, L3B: L3B}.get(a)
                for what, j in order.split():
                    j = int(j)
                    if what == "T":
                        tr(i, l, j)
                    elif what == "J":
                        pj(i, l, j)
                    elif what == "O":
                        single(i, a, j)
                    elif what == "F":
                        group(i, f, j)
                    else:
                        early(i, f, j)

            def early(i, a, j):
                if j == 0:
                    if a == L3B:
                        pe.wait_ge(glo_done, i * NB + BPC)
                    else:
                        pe.wait_ge(rlo_done, i * LNS + a + BPC)
                        pe.wait_ge(alo_done, i * NT + NT)
                for m in range(BPC):
                    agg(i, a, m, j)

            AFTER = {8: [(tr, 0)], 9: [(tr, 1)], 10: [(pj, 0)], 11: [(tr, 2), (pj, 1)],
                     12: [(tr, 3), (pj, 2)], 13: [(pj, 3)]}
            for j in range(NB):
                tr(0, 0, j)
            with pe.Fori(0, B) as i:
                for j in range(NB):
                    pj(i, 0, j)
                for v in range(4):
                    db, c = v // 2, v % 2
                    if v >= 2:
                        pe.wait_ge(rlo_done, i * LNS + NB - 3 + v)
                    for fb in range(FB):
                        last = three(ps[:, T_BANKS[v]], wm[0][:, fb, blk(db)], wm[1][:, fb, blk(db)],
                                     ht_hi[:, fb, chunk(c)], ht_lo[:, fb, chunk(c)], fb == 0, fb == FB - 1)
                    last.then_inc(tp_done, 1)
                score(i, 0)
                score(i, 1)
                pe.wait_ge(rlo_done, i * LNS + NB)
                for t in range(NT):
                    if t + 2 < NT:
                        score(i, t + 2)
                    weigh(i, t)
                    for what, j in AFTER.get(t, ()):
                        what(i, 1, j)
                run(i, 1, L0, TAIL_PE)
                run(i, 2, L1, BLOCKS_PE + " F0 T7 J6 F1 F2 J7 F3 F4 F5 F6 F7")
                run(i, 3, L2, BLOCKS_PE + " T7 J6 J7")

                def gh(k):
                    if k < 2:
                        pe.wait_ge(rlo_done, i * LNS + LNS - 1 + k)
                    if k >= 2:
                        pe.wait_ge(own_done, i * NB + k - 1)
                    for fb in range(FB):
                        last = three(ps[:, GH_BANKS[k % 2]], ht_hi[:, fb, blk(k)], ht_lo[:, fb, blk(k)],
                                     wk10[0][:, fb], wk10[1][:, fb], fb == 0, fb == FB - 1)
                    last.then_inc(gh_done, 1)

                pe.wait_ge(htlo_done, i * LNS + LNS)
                for c in range(2):
                    for fb in range(FB):
                        last = three(ps[:, SI_BANKS[c]], wui[0][:, fb], wui[1][:, fb], ht_hi[:, fb, chunk(c)],
                                     ht_lo[:, fb, chunk(c)], fb == 0, fb == FB - 1)
                    last.then_inc(si_done, 1)
                gh(0)
                gh(1)
                pe.wait_ge(rlo_done, i * LNS + LNS)
                for t in range(NT):
                    if t + 2 < NB:
                        gh(t + 2)
                    c, m = divmod(t, NB)
                    pe.wait_ge(wlo_done, i * NT + t + 1)
                    for j in range(c * BPC, (c + 1) * BPC):
                        agg(i, L3A, m, j)
                pe.wait_ge(own_done, i * NB + NB)
                pe.wait_ge(si_read, i * 4 + 4)
                run(i, NEXT, L3B, LAST_PE)


def kernel(x, adj, L0_gnn_Wq_w, L0_gnn_Wq_b, L0_gnn_Wk_w, L0_gnn_Wk_b, L0_gnn_Wv_w, L0_gnn_Wv_b,
           L1_gnn_w, L2_gnn_W, L3_gnn_Wv, L3_gnn_bv, L3_gnn_aw, L3_gnn_ab, L3_gnn_Wk, L3_gnn_bk):
    import numpy as np
    import concourse.bacc as bacc
    from concourse.bass_utils import run_bass_kernel_spmd

    def col(v):
        return np.asarray(v).reshape(-1, P).T

    def row(v):
        return np.asarray(v).reshape(1, -1)

    Wk, W2 = np.asarray(L3_gnn_Wk), np.asarray(L2_gnn_W)
    arrays = {
        "x": x,
        "adjT": np.asarray(adj).transpose(0, 2, 1),
        "wq": L0_gnn_Wq_w, "wk": L0_gnn_Wk_w,
        "bq": col(L0_gnn_Wq_b), "bk": col(L0_gnn_Wk_b),
        "wvT": np.asarray(L0_gnn_Wv_w).T, "bv": row(L0_gnn_Wv_b),
        "w1": L1_gnn_w,
        "w2": np.concatenate([W2[:, D:].T, W2[:, :D].T], axis=1),
        "wv3T": np.asarray(L3_gnn_Wv).T, "bv3": col(L3_gnn_bv),
        "aw": np.asarray(L3_gnn_aw).reshape(2, FB, P).transpose(2, 0, 1), "ab": row(L3_gnn_ab),
        "wk2": Wk[2], "wk10": np.concatenate([Wk[1], Wk[0]], axis=1),
        "bk3": L3_gnn_bk,
    }
    nc = bacc.Bacc("TRN2", target_bir_lowering=False, num_devices=1)
    arrays = {f"{n}_dram": np.ascontiguousarray(a) for n, a in arrays.items()}
    args = [nc.dram_tensor(n, a.shape, mybir.dt.from_np(a.dtype), kind="ExternalInput").ap()
            for n, a in arrays.items()]
    out = nc.dram_tensor("out_dram", (B, N, D), F32, kind="ExternalOutput").ap()
    gnn_program(nc, *args, out)
    r = run_bass_kernel_spmd(nc, [arrays], core_ids=[0])
    return r.results[0]["out_dram"]
```

```python
from contextlib import ExitStack

import concourse.bass as bass
from concourse import mybir

F32 = mybir.dt.float32
F32R = mybir.dt.float32r
ALU = mybir.AluOpType
ACT = mybir.ActivationFunctionType

P = 128
B, N, D = 8, 1024, 256
NB = N // P
FB = D // P
CH = 512
BPC = CH // P
NT = NB * (N // CH)
NV = NT // 2
RW = D + 2
ACCS = 4
S_BANK = 4
HRING = 3
R3_RING = 3
RING = 3
LN_EPS, DEG_EPS, SUM_EPS = 1e-5, 1e-6, 1e-12

LNS = 4 * NB
RES = 5 * NB
ENDS = {0: BPC, BPC: BPC + 1, BPC + 1: NB}
DEN = NB + len(ENDS)
RDEN = 2 * len(ENDS) + 1
L0, L1, L2, L3A, L3B = (NB * k for k in range(5))


BLOCKS_PE = "O4 T0 O5 T1 J0 O6 T2 J1 T3 J2 O7 T4 J3 T5 J4 F0 T6 J5 F1 T7 J6 F2 J7 F3 F4 F5 F6 F7"
BLOCKS_ACT = "N0 H0 N1 N2 H1 R0 N3 H2 R1 N4 H3 R2 N5 H4 R3 N6 H5 R4 H6 R5 N7 H7 R6 R7"
BLOCKS_DVE = ("X0 S0 X1 S1 X2 S2 H0 X3 S3 H1 X4 S4 R0 H2 R1 X5 S5 H3 X6 S6 R2 H4 R3 X7 S7 H5 R4 H6 R5 "
              "H7 R6 R7 Q0")
WEIGHTS_PE = ("O4 T0 O5 T1 J0 O6 T2 J1 I0 T3 J2 T4 I1 O7 J3 I2 T5 I3 G0 J4 G1 T6 J5 I4 T7 J6 G2 I5 J7 "
              "G3 I6 G4 I7 G5 V0 G6 V1 V2 V3 G7 V4 V5 V6 V7")
WEIGHTS_ACT = ("N0 H0 N1 N2 H1 R0 N3 H2 R1 N4 H3 R2 N5 H4 R3 N6 C0 N7 H5 G0 R4 H6 E0 H7 G1 R5 R6 E1 W0 "
               "G2 R7 E2 C1 W1 G3 G4 E3 W2 G5 E4 W3 E5 W4 G6 E6 W5 G7 E7 W6 W7 K0 K1 K2 K3")
WEIGHTS_DVE = ("X0 S0 X1 S1 X2 S2 H0 X3 S3 H1 X4 S4 R0 H2 R1 X5 S5 H3 X6 S6 R2 H4 X7 S7 R3 L0 H5 R4 H6 "
               "L1 H7 P0 R5 R6 L2 P1 R7 L3 P2 L4 P3 L5 P4 L6 P5 L7 P6 D0 Y0 Y1 Y2 Y3 P7")
WEIGHTS_POOL = ("N0 N1 N2 N3 R0 N4 R1 N5 R2 N6 R3 N7 R4 R5 W0 R6 R7 W1 W2 W3 W4 W5 W6 W7 S0 S1 S2 S3 S4 "
                "K4 K5 K6 K7 S5 S6 S7 B0 B1")
TAIL_PE = "E0 E1 T4 E2 T5 E3 J4 T6 J5 T7 F4 J6 F5 J7 F6 F7"
TAIL_ACT = "N4 N5 H4 N6 H5 N7 R4 H6 R5 H7 R6 R7"
TAIL_DVE = "X4 S4 X5 X6 S5 X7 S6 S7 H4 H5 R4 H6 R5 H7 R6 R7"
FIRST_ACT = "N0 N1 N2 H0 H1 N3 H2 N4 H3 N5 H4 N6 H5 N7 H6 H7"
LAST_PE = "T0 T1 E0 E1 E2 T2 E3 T3 F4 T4 F5 T5 F6 T6 F7 T7 O4 t0 t1 O5 t2 O6 t3 O7"
LAST_ACT = "N0 N1 N2 H0 H1 K4 K5 K6 K7 N3 H2 N4 H3 N5 H4 N6 H5 N7 H6 H7 t0 t1 t2 t3"
LAST_DVE = ("S0 S1 S2 K0 K1 K2 K3 S3 S4 D4 Y4 D5 Y5 H0 Y6 Y7 H1 S5 H2 S6 H3 S7 H4 H5 H6 X0 H7 X1 X2 "
            "X3 X4 t0 t1 X5 t2 X6 t3 X7")


def gnn_program(nc, x_d, adjT_d, Wq_d, Wk_d, bq_d, bk_d, WvT_d, bv_d, w1_d, w2_d,
                wv3T_d, bv3_d, aw_d, ab_d, wk2_d, wk10_d, bk3_d, out_d):
    ctx = ExitStack()
    with ctx:
        def sb(name, shape, dt=F32):
            return ctx.enter_context(nc.sbuf_tensor(name, shape, dt))

        def sem(name):
            return ctx.enter_context(nc.semaphore(name))

        KB = 1024
        base = -(-nc.sbuf_base // 32) * 32
        sb("slab", [P, 108 * KB // 4])

        def at(name, shape, dt, off):
            return nc.alloc_sbuf_tensor_at(name, shape, dt, offset=base + off)

        a_hi = at("a_hi", [P, NB, N], F32R, 0)
        a_lo = at("a_lo", [P, NB, N], F32R, 32 * KB)
        a_work = at("a_work", [P, NB, N], F32, 32 * KB)
        t_hi = at("t_hi", [P, FB, N], F32R, 64 * KB)
        t_lo = at("t_lo", [P, FB, N], F32R, 72 * KB)
        terms = at("terms", [P, 7, BPC, D], F32, 64 * KB)
        G1, OWN = 0, 5
        si = at("si", [P, N], F32, 72 * KB)
        si2 = at("si2", [P, N], F32, 76 * KB)
        r3 = at("r3", [P, R3_RING, D + 2], F32, 80 * KB)
        p_hi = at("p_hi", [P, RING, CH], F32R, 80 * KB)
        p_lo = at("p_lo", [P, RING, CH], F32R, 86 * KB)
        p_work = at("p_work", [P, RING, CH], F32, 86 * KB)
        ht_hi = at("ht_hi", [P, FB, N], F32R, 92 * KB)
        ht_lo = at("ht_lo", [P, FB, N], F32R, 100 * KB)
        wq_raw = at("wq_raw", [P, FB, D], F32, 0)
        wk_raw = at("wk_raw", [P, FB, D], F32, 2 * KB)
        wv_raw = at("wv_raw", [P, FB, D], F32, 32 * KB)
        w1_raw = at("w1_raw", [P, FB, D], F32, 34 * KB)
        wv3_raw = at("wv3_raw", [P, FB, D], F32, 8 * KB)
        wk2_raw = at("wk2_raw", [P, FB, D], F32, 36 * KB)
        w2_raw = at("w2_raw", [P, FB, 2 * D], F32, 38 * KB)
        wk10_raw = at("wk10_raw", [P, FB, 2 * D], F32, 42 * KB)
        bk3_raw = at("bk3_raw", [P, 3, D], F32, 46 * KB)
        bq_raw = at("bq_raw", [P, FB], F32, 23 * KB)
        bk_raw = at("bk_raw", [P, FB], F32, 23 * KB + 32)
        bv3_raw = at("bv3_raw", [P, FB], F32, 23 * KB + 64)
        aw_raw = at("aw_raw", [P, 2, FB], F32, 23 * KB + 96)
        ab_raw = at("ab_raw", [P, 1], F32, 23 * KB + 128)
        bb = at("bb", [P, 2, FB], F32, 23 * KB + 160)
        aws = at("aws", [P, FB], F32, 23 * KB + 192)
        ones = at("ones", [P, P], F32, 24 * KB)
        sums = at("sums", [P, 2], F32, 25 * KB)
        bk_two = at("bk_two", [P, D], F32, 49 * KB)

        x_in = sb("x_in", [P, NB, D])
        x = sb("x", [P, NB, D])
        r_hi = [sb(f"r{k}_hi", [P, NB, RW], F32R) for k in range(2)]
        r_lo = [sb(f"r{k}_lo", [P, NB, RW], F32R) for k in range(2)]
        adj_in = sb("adj_in", [P, 2, 2, CH])
        wm = [sb(f"wm_{s}", [P, FB, D], F32R) for s in ("hi", "lo")]
        wv = [sb(f"wv_{s}", [P, FB, RW], F32R) for s in ("hi", "lo")]
        w1 = [sb(f"w1_{s}", [P, FB, D], F32R) for s in ("hi", "lo")]
        w2 = [sb(f"w2_{s}", [P, FB, 2 * D], F32R) for s in ("hi", "lo")]
        wk2 = [sb(f"wk2_{s}", [P, FB, RW], F32R) for s in ("hi", "lo")]
        wk10 = [sb(f"wk10_{s}", [P, FB, 2 * D], F32R) for s in ("hi", "lo")]
        bv_row = sb("bv_row", [P, D])
        bk_row = sb("bk_row", [P, D])
        h = sb("h", [P, HRING, D])
        u = sb("u", [P, 2, D])
        ident = sb("ident", [P, P])
        bn = sb("bn", [P, NB, 6])
        mv = sb("mv", [P, NB, 2])
        ve = sb("ve", [P, NB])
        rstd = sb("rstd", [P, NB])
        nmr = sb("nmr", [P, NB])
        minus_half = sb("minus_half", [P, 1])
        tc = sb("tc", [P, FB])
        g0 = sb("g0", [P, 1])
        s0 = sb("s0", [P, 1])
        g = sb("g", [P, NB])
        sj8 = sb("sj8", [P, NB])
        sj2 = sb("sj2", [P, NB])
        den = sb("den", [P, NB])
        rden = sb("rden", [P, NB])
        ps = ctx.enter_context(nc.psum_tensor("ps", [P, 8, CH], F32))

        passed_sp, passed_v, passed_p = sem("passed_sp"), sem("passed_v"), sem("passed_p")
        w_loaded, w_more_loaded = sem("w_loaded"), sem("w_more_loaded")
        x_loaded, stored = sem("x_loaded"), sem("stored")
        adj_loaded = [sem("adj_loaded0"), sem("adj_loaded1")]
        setup_v, setup_p, setup_a, setup_pe = sem("setup_v"), sem("setup_p"), sem("setup_a"), sem("setup_pe")
        bn_done, mv_done = sem("bn_done"), sem("mv_done")
        ve_done, rstd_done, nmr_done = sem("ve_done"), sem("rstd_done"), sem("nmr_done")
        xb_done = sem("xb_done")
        h_done, hthi_done = sem("h_done"), sem("hthi_done")
        tr_done = sem("tr_done")
        htlo_done = sem("htlo_done")
        pj_done, rhi_done, rlo_done = sem("pj_done"), sem("rhi_done"), sem("rlo_done")
        tp_done, thi_done, tlo_done = sem("tp_done"), sem("thi_done"), sem("tlo_done")
        s_done, exp_done, mul_done = sem("s_done"), sem("exp_done"), sem("mul_done")
        phi_done, plo_done, pv_done = sem("phi_done"), sem("plo_done"), sem("pv_done")
        ahi_done, alo_done = sem("ahi_done"), sem("alo_done")
        res_done, res_read = sem("res_done"), sem("res_read")
        den_done, rden_done, x2_done, out_done = sem("den_done"), sem("rden_done"), sem("x2_done"), sem("out_done")
        si_done, si_read = sem("si_done"), sem("si_read")
        leaky_done, e3_done = sem("leaky_done"), sem("e3_done")
        mul3_done, whi_done, wlo_done = sem("mul3_done"), sem("whi_done"), sem("wlo_done")
        r3_done, sj_done = sem("r3_done"), sem("sj_done")
        gh_done, g1_done, own_done = sem("gh_done"), sem("g1_done"), sem("own_done")
        ghi_done, glo_done, glo_late_done = sem("ghi_done"), sem("glo_done"), sem("glo_late_done")

        SETUP_BB = 2 + 2 + 1 + 3
        SETUP_T = SETUP_BB + (2 + 1 + 2) * FB
        SETUP_V = SETUP_T + 2 * FB + 4
        SETUP_P = 3 + 5 + 2
        WEIGHTS = ((wv, wv_raw), (w1, w1_raw), (w2, w2_raw), (wk2, wk2_raw), (wk10, wk10_raw))
        R_OF = {L0: 0, L1: 1, L2: 0, L3A: 1, L3B: 0}
        N_W, N_W_MORE = 8, 7

        def tr_bank(l, j):
            return 7 if j % 2 == 0 or (l == 1 and j < BPC) else 5

        def pj_bank(l, j):
            if l == 0:
                return (6, 7)[j % 2]
            return 6 if j % 2 == 0 or (l == 1 and j < BPC) else 4

        def last_use(bank, l, j):
            q = l * NB + j
            return next((p + 1 for p in range(q - 1, -1, -1) if bank(*divmod(p, NB)) == bank(l, j)), 0)

        T_BANKS = (7, 5, 7, 5)
        SI_BANKS = (0, 1)
        GH_BANKS = (2, 3, 7, 6, 5, 4, 7, 6)
        NEXT = 4

        def term(which, j):
            return terms[:, which + j // BPC, j % BPC]

        def bank_of(k):
            return slice(k.start % ACCS, k.start % ACCS + k.stop - k.start)

        def blk(j):
            return slice(j * P, (j + 1) * P)

        def pair(v):
            c, m = v // (NB // 2), v % (NB // 2) * 2
            return slice(m, m + 2), chunk(c)

        def chunk(c):
            return slice(c * CH, (c + 1) * CH)

        block = ctx.enter_context(nc.Block())

        @block.sync
        def _(sp):
            def halves(w):
                return w.rearrange("(a p) n -> p a n", p=P)

            def load_x(i):
                sp.dma_start(x_in[:], x_d[bass.ds(i, 1)].rearrange("b (j p) d -> p (b j) d", p=P)
                             if not isinstance(i, int) else
                             x_d[i].rearrange("(j p) d -> p j d", p=P)).then_inc(x_loaded, 16)

            def load_adj(i, s):
                c, pair_of = s % 8 // 4, s % 4
                src = adjT_d[i] if isinstance(i, int) else adjT_d[bass.ds(i, 1)]
                if isinstance(i, int):
                    src = src.rearrange("(a m p) n -> a p m n", m=2, p=P)[pair_of][:, :, chunk(c)]
                else:
                    src = src.rearrange("b (a m p) n -> a p (b m) n", m=2, p=P)[pair_of][:, :, chunk(c)]
                sp.dma_start(adj_in[:, s % 2], src).then_inc(adj_loaded[s % 2], 16)

            def freed(i, s):
                if s <= 9:
                    sp.wait_ge(mul_done, i * NT + 2 * (s - 1))
                    sp.sem_inc(passed_sp, 1)
                    sp.wait_ge(alo_done, i * NV + s - 1)
                else:
                    sp.wait_ge(mul3_done, i * NV + s - 9)
                sp.sem_inc(passed_sp, 1)

            def graph(i, more):
                for s in range(2, 8):
                    freed(i, s)
                    load_adj(i, s)
                sp.wait_ge(res_read, i * RES + L1)
                sp.sem_inc(passed_sp, 1)
                load_x(i + 1 if more else i)
                for s in range(8, 16):
                    freed(i, s)
                    load_adj(i, s)
                if more:
                    for s in range(16, 18):
                        freed(i, s)
                        load_adj(i + 1, s - 16)

            for dst, src in (
                (wk_raw[:], halves(Wk_d)), (wq_raw[:], halves(Wq_d)), (bq_raw[:], bq_d), (bk_raw[:], bk_d),
                (wv3_raw[:], halves(wv3T_d)), (bv3_raw[:], bv3_d), (aw_raw[:], aw_d),
                (ab_raw[:], ab_d.partition_broadcast(P)),
            ):
                sp.dma_start(dst, src).then_inc(w_loaded, 16)
            load_x(0)
            for k, (dst, src) in enumerate((
                (wv_raw[:], halves(WvT_d)), (bv_row[:], bv_d.partition_broadcast(P)),
                (w1_raw[:], halves(w1_d)), (w2_raw[:], halves(w2_d)), (wk2_raw[:], halves(wk2_d)),
                (wk10_raw[:], halves(wk10_d)), (bk3_raw[:], bk3_d.partition_broadcast(P)),
            )):
                sp.dma_start(dst, src).then_inc(w_more_loaded, 16)
                if k == 1:
                    for s in range(2):
                        load_adj(0, s)
            with sp.Fori(0, B - 1) as i:
                graph(i, True)
            graph(B - 1, False)

        @block.gpsimd
        def _(pool):
            gp = nc.gpsimd
            gp.memset(ident[:], 0.0).then_inc(setup_p, 1)
            gp.memset(minus_half[:], -0.5).then_inc(setup_p, 1)
            pool.wait_ge(setup_p, 2)
            gp.affine_select(out=ident[:], in_=ident[:], compare_op=ALU.not_equal, fill=1.0, base=0,
                             pattern=[[-1, P]], channel_multiplier=1).then_inc(setup_p, 1)

            def rstds(i, l, j):
                q = l * NB + j + 1
                pool.wait_ge(mv_done, i * LNS + q)
                pool.sem_inc(passed_p, 1)
                gp.tensor_scalar(ve[:, j:j + 1], mv[:, j, 1:2], LN_EPS, 1.0, ALU.add, ALU.mult).then_inc(ve_done, 1)
                pool.wait_ge(ve_done, i * LNS + q)
                gp.tensor_tensor(rstd[:, j:j + 1], ve[:, j:j + 1], minus_half[:], ALU.pow).then_inc(rstd_done, 1)
                pool.wait_ge(rstd_done, i * LNS + q)
                pool.sem_inc(passed_p, 1)
                gp.tensor_scalar(nmr[:, j:j + 1], mv[:, j, 0:1], rstd[:, j:j + 1], -1.0,
                                 ALU.mult, ALU.mult).then_inc(nmr_done, 1)

            def split_adj(i, v):
                mb, n = pair(v)
                pool.wait_ge(ahi_done, i * NV + v + 1)
                gp.tensor_tensor(a_lo[:, mb, n], adj_in[:, v % 2], a_hi[:, mb, n].bitcast(F32),
                                 ALU.subtract).then_inc(alo_done, 1)

            def w_split(i, v):
                mb, n = pair(v)
                pool.wait_ge(whi_done, i * NV + v + 1)
                gp.tensor_tensor(a_lo[:, mb, n], a_work[:, mb, n], a_hi[:, mb, n].bitcast(F32),
                                 ALU.subtract).then_inc(wlo_done, 1)

            def split_r(i, j):
                pool.wait_ge(rhi_done, i * LNS + 3 * NB + j + 1)
                gp.tensor_tensor(r_lo[1][:, j, 0:D], r3[:, j % R3_RING, 0:D], r_hi[1][:, j, 0:D].bitcast(F32),
                                 ALU.subtract).then_inc(rlo_done, 1)

            def own3(i, c):
                pool.wait_ge(g1_done, i * NB + (c + 1) * BPC)
                gp.tensor_tensor(terms[:, OWN + c], terms[:, OWN + c],
                                 bk_row[:].unsqueeze(1).broadcast_to([P, BPC, D]), ALU.add).then_inc(own_done, 1)

            def split_g(i, j):
                pool.wait_ge(ghi_done, i * NB + j + 1)
                gp.tensor_tensor(r_lo[0][:, j, 0:D], term(G1, j), r_hi[0][:, j, 0:D].bitcast(F32),
                                 ALU.subtract).then_inc(glo_late_done, 1)

            for j in range(NB):
                rstds(0, 0, j)
            steps = [3]

            def link(ins):
                steps[0] += 1
                ins.then_inc(setup_p, 1)
                pool.wait_ge(setup_p, steps[0])

            pool.wait_ge(w_more_loaded, 16 * N_W_MORE)
            for k, ((hi, lo), raw) in enumerate(WEIGHTS):
                width = raw.shape[2]
                pool.wait_ge(setup_a, k + 1)
                link(gp.tensor_tensor(lo[:, :, 0:width], raw[:], hi[:, :, 0:width].bitcast(F32), ALU.subtract))
            link(gp.tensor_tensor(bk_two[:], bk3_raw[:, 0], bk3_raw[:, 1], ALU.add))
            link(gp.tensor_tensor(bk_row[:], bk_two[:], bk3_raw[:, 2], ALU.add))
            assert steps[0] == SETUP_P
            with pool.Fori(0, B) as i:
                for v in range(NV):
                    split_adj(i, v)
                    for j in range(2 * v, min(2 * v + 2, NB)):
                        pool.wait_ge(h_done, i * LNS + j + 1)
                        gp.tensor_tensor(x_in[:, j], x_in[:, j], bv_row[:], ALU.add).then_inc(xb_done, 1)
                    for j in {4: (0, 1, 2), 5: (3,)}.get(v, ()):
                        rstds(i, 1, j)
                for j in range(BPC, NB):
                    rstds(i, 1, j)
                for j in range(NB):
                    rstds(i, 2, j)
                for what, j in WEIGHTS_POOL.split():
                    if what == "S":
                        rstds(i, NEXT, int(j))
                    else:
                        {"N": lambda i, j: rstds(i, 3, j), "R": split_r, "W": w_split, "B": own3,
                         "K": split_g}[what](i, int(j))

        @block.scalar
        def _(act):
            sc = nc.scalar

            def norm(i, l, j):
                q = l * NB + j + 1
                act.wait_ge(nmr_done, i * LNS + q)
                if q > HRING:
                    act.wait_ge(tr_done, i * LNS + q - HRING)
                src = x_in if l in (0, NEXT) else x
                sc.activation(h[:, (q - 1) % HRING], src[:, j], ACT.Relu, bias=nmr[:, j:j + 1],
                              scale=rstd[:, j:j + 1]).then_inc(h_done, 1)

            def ht(i, l, j):
                act.wait_ge(tr_done, i * LNS + l * NB + j + 1)
                sc.copy(ht_hi[:, :, blk(j)],
                        ps[:, tr_bank(l, j), 0:D].rearrange("p (a n) -> p a n", a=FB)).then_inc(hthi_done, 1)

            def right(i, l, j):
                k = l % 2
                act.wait_ge(pj_done, i * LNS + l * NB + j + 1)
                if l == 2:
                    sc.copy(term(OWN, j), ps[:, pj_bank(l, j), D:2 * D])
                if l == 3:
                    if j >= R3_RING:
                        act.wait_ge(rlo_done, i * LNS + l * NB + j - R3_RING + 1)
                        act.wait_ge(sj_done, i * NB + j - R3_RING + 1)
                        act.wait_ge(si_done, i * NB + j - R3_RING + 1)
                    sc.copy(r3[:, j % R3_RING], ps[:, pj_bank(l, j), 0:D + 2]).then_inc(r3_done, 1)
                sc.copy(r_hi[k][:, j, 0:D], ps[:, pj_bank(l, j), 0:D]).then_inc(rhi_done, 1)

            def adj_hi(i, v):
                mb, n = pair(v)
                act.wait_ge(adj_loaded[v % 2], i * 128 + 16 * (v // 2 + 1))
                sc.copy(a_hi[:, mb, n], adj_in[:, v % 2]).then_inc(ahi_done, 1)

            def t_split(i, l, v):
                db, c = v // 2, v % 2
                act.wait_ge(tp_done, i * 4 + l + v + 1)
                sc.activation(t_hi[:, db, chunk(c)], ps[:, T_BANKS[v]], ACT.Identity,
                              bias=tc[:, db:db + 1]).then_inc(thi_done, 1)

            def weighed(i, t):
                c, m = divmod(t, NB)
                if m == NB - 1:
                    act.wait_ge(res_done, i * RES + (c + 1) * BPC)
                else:
                    act.wait_ge(pv_done, i * (NT - 2) + t - c + 1)

            def expo(i, t):
                m = t % NB
                if t < NB:
                    act.wait_ge(rlo_done, i * LNS + t + 1)
                act.wait_ge(s_done, i * NT + t + 1)
                if t >= RING:
                    weighed(i, t - RING)
                sc.activation(p_work[:, t % RING], ps[:, S_BANK + t % 2], ACT.Exp,
                              bias=g[:, m:m + 1]).then_inc(exp_done, 1)

            def p_split(i, t):
                act.wait_ge(mul_done, i * NT + t + 1)
                sc.copy(p_hi[:, t % RING], p_work[:, t % RING]).then_inc(phi_done, 1)

            def si_copy(i, c):
                act.wait_ge(si_done, i * NB + (c + 1) * BPC)
                sc.copy(si[:, chunk(c)], ps[:, SI_BANKS[c]]).then_inc(si_read, 1)
                sc.mul(si2[:, chunk(c)], ps[:, SI_BANKS[c]], 0.2).then_inc(si_read, 1)

            def exp3(i, v):
                mb, n = pair(v)
                act.wait_ge(sj_done, i * NB + mb.stop)
                for m in range(mb.start, mb.stop):
                    act.wait_ge(leaky_done, i * NT + 2 * v + m - mb.start + 1)
                    sc.activation(a_work[:, m, n], a_work[:, m, n], ACT.Exp,
                                  bias=sj2[:, m:m + 1]).then_inc(e3_done, 1)

            def w_split(i, v):
                mb, n = pair(v)
                act.wait_ge(mul3_done, i * NV + v + 1)
                sc.copy(a_hi[:, mb, n], a_work[:, mb, n]).then_inc(whi_done, 1)

            def g1_copy(i, k):
                act.wait_ge(gh_done, i * NB + k + 1)
                sc.copy(terms[:, k // BPC:k // BPC + OWN + 1:OWN, k % BPC],
                        ps[:, GH_BANKS[k]].rearrange("p (a n) -> p a n", a=2)).then_inc(g1_done, 1)

            def g_split(i, j):
                act.wait_ge(res_read, i * RES + L3A + j + 1)
                sc.copy(r_hi[0][:, j, 0:D], term(G1, j)).then_inc(ghi_done, 1)

            AFTER = {9: [(norm, 0)], 10: [(norm, 1), (norm, 2)], 11: [(ht, 0)],
                     12: [(ht, 1), (right, 0), (norm, 3)], 13: [(ht, 2), (right, 1)],
                     14: [(ht, 3), (right, 2)], 15: [(right, 3)]}
            steps = {"N": norm, "H": ht, "R": right, "C": lambda i, l, c: si_copy(i, c),
                     "E": lambda i, l, v: exp3(i, v),
                     "W": lambda i, l, v: w_split(i, v), "G": lambda i, l, k: g1_copy(i, k),
                     "K": lambda i, l, j: g_split(i, j), "t": t_split}
            for what, j in FIRST_ACT.split():
                steps[what](0, 0, int(j))
            act.wait_ge(w_more_loaded, 16 * N_W_MORE)
            for (hi, lo), raw in WEIGHTS:
                sc.copy(hi[:, :, 0:raw.shape[2]], raw[:]).then_inc(setup_a, 1)
            act.wait_ge(setup_v, SETUP_T)
            for v in range(4):
                t_split(0, 0, v)
            act.wait_ge(setup_v, SETUP_V)
            with act.Fori(0, B) as i:
                right(i, 0, 0)
                right(i, 0, 1)
                expo(i, 0)
                adj_hi(i, 0)
                for t in range(NT):
                    if t + 1 < NT:
                        expo(i, t + 1)
                    if t == 0:
                        right(i, 0, 2)
                    p_split(i, t)
                    if t % 2 == 1 and t + 1 < NT:
                        adj_hi(i, (t + 1) // 2)
                    if t < 5:
                        right(i, 0, t + 3)
                    for what, j in AFTER.get(t, ()):
                        what(i, 1, j)
                for l, order in ((1, TAIL_ACT), (2, BLOCKS_ACT), (3, WEIGHTS_ACT)):
                    for what, j in order.split():
                        steps[what](i, l, int(j))
                for what, j in LAST_ACT.split():
                    steps[what](i, NEXT, int(j))
                for c in range(2):
                    act.wait_ge(out_done, i * NB + (c + 1) * BPC)
                    act.dma_start(out_d[bass.ds(i, 1)].rearrange("b (c j p) d -> c p (b j) d", c=2, p=P)[c],
                                  x[:, c * BPC:(c + 1) * BPC]).then_inc(stored, 16)
            act.wait_ge(stored, 16 + 32 * B)

        @block.vector
        def _(dve):
            ve_ = nc.vector
            steps = [0]

            def link(ins):
                steps[0] += 1
                ins.then_inc(setup_v, 1)
                dve.wait_ge(setup_v, steps[0])

            def split(w, dst, src):
                link(ve_.tensor_copy(dst(w[0]), src))
                link(ve_.tensor_tensor(dst(w[1]), src, dst(w[0]).bitcast(F32), ALU.subtract))

            for k in range(2):
                ve_.memset(r_hi[k][:, :, D:D + 1].bitcast(F32), 1.0)
                ve_.memset(r_hi[k][:, :, D + 1:RW].bitcast(F32), 0.0)
                link(ve_.memset(r_lo[k][:, :, D:RW].bitcast(F32), 0.0))
            for w in wv:
                link(ve_.memset(w[:, :, D:RW].bitcast(F32), 0.0))
            link(ve_.memset(ones[:], 1.0))
            def stats(i, l, j):
                q = l * NB + j + 1
                if l in (0, NEXT):
                    if j == 0:
                        dve.wait_ge(x_loaded, i * 16 + (16 if l == 0 else 32))
                elif l == 3:
                    dve.wait_ge(x2_done, i * NB + j + 1)
                else:
                    dve.wait_ge(res_read, i * RES + (l - 1) * NB + j + 1)
                src = x_in if l in (0, NEXT) else x
                ve_.bn_stats(bn[:, j], src[:, j]).then_inc(bn_done, 1)
                dve.wait_ge(bn_done, i * LNS + q)
                dve.sem_inc(passed_v, 1)
                ve_.bn_aggr(mv[:, j], bn[:, j]).then_inc(mv_done, 1)

            def ht(i, l, j):
                dve.wait_ge(hthi_done, i * LNS + l * NB + j + 1)
                ve_.tensor_tensor(ht_lo[:, :, blk(j)], ps[:, tr_bank(l, j), 0:D].rearrange("p (a n) -> p a n", a=FB),
                                  ht_hi[:, :, blk(j)].bitcast(F32), ALU.subtract).then_inc(htlo_done, 1)

            def right(i, l, j):
                k = l % 2
                dve.wait_ge(rhi_done, i * LNS + l * NB + j + 1)
                last = ps[:, pj_bank(l, j), D:D + 1]
                if l == 0:
                    ve_.tensor_scalar(g[:, j:j + 1], last, g0[:], None, ALU.add)
                ve_.tensor_tensor(r_lo[k][:, j, 0:D], ps[:, pj_bank(l, j), 0:D],
                                  r_hi[k][:, j, 0:D].bitcast(F32), ALU.subtract).then_inc(rlo_done, 1)

            def right3(i, j):
                dve.wait_ge(r3_done, i * NB + j + 1)
                last = r3[:, j % R3_RING, D:D + 1]
                ve_.tensor_scalar(sj8[:, j:j + 1], last, s0[:], 0.8, ALU.add, ALU.mult)
                ve_.tensor_scalar(sj2[:, j:j + 1], last, s0[:], 0.2, ALU.add, ALU.mult).then_inc(sj_done, 1)

            def res0(i, j):
                dve.wait_ge(res_done, i * RES + L0 + j + 1)
                if j in ENDS:
                    k, n = slice(j, ENDS[j]), list(ENDS).index(j)
                    dve.wait_ge(res_done, i * RES + L0 + k.stop)
                    ve_.reciprocal(rden[:, k], ps[:, bank_of(k), D]).then_inc(rden_done, 1)
                    dve.wait_ge(rden_done, i * RDEN + n + 1)
                if j == 0:
                    dve.wait_ge(stored, i * 32 + 16)
                dve.wait_ge(xb_done, i * NB + j + 1)
                ve_.scalar_tensor_tensor(out=x[:, j], in0=ps[:, j % ACCS, 0:D], scalar=rden[:, j:j + 1],
                                         in1=x_in[:, j], op0=ALU.mult, op1=ALU.add).then_inc(res_read, 1)

            def res1(i, j):
                dve.wait_ge(res_done, i * RES + L1 + j + 1)
                ve_.tensor_scalar(den[:, j:j + 1], ps[:, j % ACCS, D:D + 1], DEG_EPS, None,
                                  ALU.max).then_inc(den_done, 1)
                ve_.tensor_tensor(x[:, j], ps[:, j % ACCS, 0:D], x[:, j], ALU.add).then_inc(res_read, 1)

            def divide2(i, _):
                dve.wait_ge(den_done, i * DEN + NB)
                ve_.reciprocal(rden[:], den[:]).then_inc(rden_done, 1)

            def res2(i, j):
                dve.wait_ge(res_done, i * RES + L2 + j + 1)
                if j == 0:
                    dve.wait_ge(rden_done, i * RDEN + len(ENDS) + 1)
                ve_.scalar_tensor_tensor(out=u[:, j % 2], in0=ps[:, j % ACCS, 0:D], scalar=rden[:, j:j + 1],
                                         in1=term(OWN, j), op0=ALU.mult, op1=ALU.add).then_inc(res_read, 1)
                dve.wait_ge(res_read, i * RES + L2 + j + 1)
                ve_.scalar_tensor_tensor(out=x[:, j], in0=u[:, j % 2], scalar=0.0, in1=x[:, j],
                                         op0=ALU.max, op1=ALU.add).then_inc(x2_done, 1)

            def divide(i, j):
                k, n = slice(j, ENDS[j]), list(ENDS).index(j)
                dve.wait_ge(res_done, i * RES + L3A + k.stop)
                ve_.tensor_scalar(den[:, k], ps[:, bank_of(k), D], SUM_EPS, None, ALU.add).then_inc(den_done, 1)
                dve.wait_ge(den_done, i * DEN + NB + n + 1)
                ve_.reciprocal(rden[:, k], den[:, k]).then_inc(rden_done, 1)
                dve.wait_ge(rden_done, i * RDEN + len(ENDS) + 1 + n + 1)

            def res3a(i, j):
                ve_.scalar_tensor_tensor(out=term(G1, j), in0=ps[:, j % ACCS, 0:D], scalar=rden[:, j:j + 1],
                                         in1=term(G1, j), op0=ALU.mult, op1=ALU.add).then_inc(res_read, 1)

            def split_g(i, j):
                dve.wait_ge(ghi_done, i * NB + j + 1)
                ve_.tensor_tensor(r_lo[0][:, j, 0:D], term(G1, j), r_hi[0][:, j, 0:D].bitcast(F32),
                                  ALU.subtract).then_inc(glo_done, 1)

            def res3b(i, j):
                dve.wait_ge(res_done, i * RES + L3B + j + 1)
                dve.wait_ge(own_done, i * 2 + j // BPC + 1)
                ve_.scalar_tensor_tensor(out=u[:, j % 2], in0=ps[:, j % ACCS, 0:D], scalar=rden[:, j:j + 1],
                                         in1=term(OWN, j), op0=ALU.mult, op1=ALU.add).then_inc(res_read, 1)
                dve.wait_ge(res_read, i * RES + L3B + j + 1)
                ve_.scalar_tensor_tensor(out=x[:, j], in0=u[:, j % 2], scalar=0.0, in1=x[:, j],
                                         op0=ALU.max, op1=ALU.add).then_inc(out_done, 1)

            def adj_loads(i, s):
                dve.wait_ge(adj_loaded[s % 2], i * 128 + 16 * (s // 2 + 1))

            def product(i, t):
                c, m = divmod(t, NB)
                adj = adj_in[:, t // 2 % 2, t % 2]
                if t % 2 == 0:
                    adj_loads(i, t // 2)
                dve.wait_ge(exp_done, i * NT + t + 1)
                ve_.tensor_tensor(p_work[:, t % RING], p_work[:, t % RING], adj, ALU.mult).then_inc(mul_done, 1)

            def p_split(i, t):
                dve.wait_ge(phi_done, i * NT + t + 1)
                ve_.tensor_tensor(p_lo[:, t % RING], p_work[:, t % RING],
                                  p_hi[:, t % RING].bitcast(F32), ALU.subtract).then_inc(plo_done, 1)

            def product3(i, v):
                mb, n = pair(v)
                adj_loads(i, NV + v)
                dve.wait_ge(e3_done, i * NT + 2 * v + 2)
                ve_.tensor_tensor(a_work[:, mb, n], a_work[:, mb, n], adj_in[:, v % 2],
                                  ALU.mult).then_inc(mul3_done, 1)

            def leaky(i, v):
                mb, n = pair(v)
                dve.wait_ge(sj_done, i * NB + mb.stop)
                dve.wait_ge(si_read, i * 4 + (2 if v < NV // 2 else 4))
                for m in range(mb.start, mb.stop):
                    ve_.scalar_tensor_tensor(out=a_work[:, m, n], in0=si[:, n], scalar=sj8[:, m:m + 1],
                                             in1=si2[:, n], op0=ALU.add, op1=ALU.max).then_inc(leaky_done, 1)

            AFTER = {8: [(stats, 0)], 9: [(stats, 1), (stats, 2)], 10: [(stats, 3)], 11: [(ht, 0)],
                     12: [(ht, 1), (right, 0)], 13: [(ht, 2), (right, 1)], 14: [(ht, 3), (right, 2)],
                     15: [(right, 3)]}

            def t_split(i, l, v):
                db, c = v // 2, v % 2
                dve.wait_ge(thi_done, i * 4 + l + v + 1)
                ve_.scalar_tensor_tensor(out=t_lo[:, db, chunk(c)], in0=ps[:, T_BANKS[v]],
                                         scalar=tc[:, db:db + 1], in1=t_hi[:, db, chunk(c)].bitcast(F32),
                                         op0=ALU.add, op1=ALU.subtract).then_inc(tlo_done, 1)

            dve.wait_ge(w_loaded, 16 * N_W)
            link(ve_.tensor_tensor(bb[:, 0], bq_raw[:], bk_raw[:], ALU.mult))
            link(ve_.tensor_tensor(aws[:], aw_raw[:, 0], aw_raw[:, 1], ALU.add))
            link(ve_.tensor_tensor(bb[:, 1], bv3_raw[:], aws[:], ALU.mult))
            assert steps[0] == SETUP_BB
            for j in range(NB):
                stats(0, 0, j)
            dve.wait_ge(setup_pe, 1)
            for fb in range(FB):
                split(wm, lambda w: w[:, fb], ps[:, fb, 0:D])
                link(ve_.tensor_copy(tc[:, fb:fb + 1], ps[:, 2 + fb, 1:2]))
                ht(0, 0, 2 * fb)
                ht(0, 0, 2 * fb + 1)
            for fb in range(FB):
                split(wv, lambda w: w[:, fb, D:D + 1], ps[:, 2 + fb, 0:1])
            assert steps[0] == SETUP_T
            for j in range(4, NB):
                ht(0, 0, j)
            t_split(0, 0, 0)
            for fb in range(FB):
                split(wk2, lambda w: w[:, fb, D:D + 2], ps[:, 2 + fb, 2:4])
            t_split(0, 0, 1)
            link(ve_.tensor_copy(sums[:, 0:1], ps[:, 4, 0:1]))
            link(ve_.tensor_copy(sums[:, 1:2], ps[:, 4, 1:2]))
            link(ve_.tensor_copy(g0[:], sums[:, 0:1]))
            link(ve_.tensor_tensor(s0[:], sums[:, 1:2], ab_raw[:], ALU.add))
            assert steps[0] == SETUP_V
            t_split(0, 0, 2)
            t_split(0, 0, 3)
            ve_.memset(u[:, 0, 0:1], 0.0).then_inc(stored, 16)
            with dve.Fori(0, B) as i:
                right(i, 0, 0)
                right(i, 0, 1)
                product(i, 0)
                right(i, 0, 2)
                for t in range(NT):
                    if t + 1 < NT:
                        product(i, t + 1)
                    p_split(i, t)
                    if t < 5:
                        right(i, 0, t + 3)
                    if t == NB:
                        for j in range(BPC):
                            res0(i, j)
                    for what, j in AFTER.get(t, ()):
                        what(i, 1, j)
                for l, res, order in ((1, res0, TAIL_DVE), (2, res1, BLOCKS_DVE), (3, res2, WEIGHTS_DVE)):
                    steps = {"X": res, "S": lambda i, j: stats(i, l, j), "H": lambda i, j: ht(i, l, j),
                             "R": right3 if l == 3 else lambda i, j: right(i, l, j), "L": leaky, "P": product3, "Q": divide2, "D": divide, "Y": res3a}
                    for what, j in order.split():
                        steps[what](i, int(j))
                for what, j in LAST_DVE.split():
                    {"K": split_g, "D": divide, "Y": res3a, "X": res3b, "S": lambda i, j: stats(i, NEXT, j),
                     "H": lambda i, j: ht(i, NEXT, j), "t": lambda i, v: t_split(i, NEXT, v)}[what](i, int(j))

        @block.tensor
        def _(pe):
            mm = nc.tensor.matmul

            pe.wait_ge(w_loaded, 16 * N_W)
            pe.wait_ge(setup_v, SETUP_BB)
            for fb in range(FB):
                for ob in range(FB):
                    mm(ps[:, fb, 0:D], wk_raw[:, ob, blk(fb)], wq_raw[:, ob], start=ob == 0, stop=ob == 1)
                for w, vec, col in ((wk_raw, bq_raw[:].unsqueeze(1), 0), (wq_raw, bk_raw[:].unsqueeze(1), 1),
                                    (wv3_raw, aw_raw[:], 2)):
                    for ob in range(FB):
                        mm(ps[:, 2 + fb, col:col + vec.shape[1]], w[:, ob, blk(fb)], vec[:, :, ob],
                           start=ob == 0 and col == 0, stop=ob == 1, skip_group_check=True)
            pe.wait_ge(setup_p, 3)
            for ob in range(FB):
                last = mm(ps[:, 4, 0:2], ones[:], bb[:, :, ob], start=ob == 0, stop=ob == 1)
            last.then_inc(setup_pe, 1)

            def three(out, a_hi_, a_lo_, b_hi, b_lo, first, last):
                mm(out, a_hi_, b_hi, start=first, stop=False)
                mm(out, a_hi_, b_lo, start=False, stop=False)
                return mm(out, a_lo_, b_hi, start=False, stop=last)

            def tr(i, l, j):
                q = l * NB + j
                pe.wait_ge(h_done, i * LNS + q + 1)
                if last_use(tr_bank, l, j):
                    pe.wait_ge(htlo_done, i * LNS + last_use(tr_bank, l, j))
                for fb in range(FB):
                    last = nc.tensor.transpose(ps[:, tr_bank(l, j), blk(fb)], h[:, q % HRING, blk(fb)], ident[:])
                last.then_inc(tr_done, 1)

            def pj(i, l, j):
                q = l * NB + j
                w = (wv, w1, w2, wk2)[l]
                width = w[0].shape[2]
                pe.wait_ge(htlo_done, i * LNS + q + 1)
                if (l, j) == (0, 1):
                    pe.wait_ge(tlo_done, i * 4 + 3)
                if l == 3 and j >= 2:
                    pe.wait_ge(rhi_done, i * LNS + last_use(pj_bank, l, j))
                elif last_use(pj_bank, l, j):
                    pe.wait_ge(rlo_done, i * LNS + last_use(pj_bank, l, j))
                if l == 1 and j == 0:
                    pe.wait_ge(setup_v, SETUP_V)
                    pe.wait_ge(setup_p, SETUP_P)
                for fb in range(FB):
                    last = three(ps[:, pj_bank(l, j), 0:width], ht_hi[:, fb, blk(j)], ht_lo[:, fb, blk(j)],
                                 w[0][:, fb], w[1][:, fb], fb == 0, fb == FB - 1)
                last.then_inc(pj_done, 1)

            def agg(i, a, m, j, wait=None):
                k = R_OF[a]
                n = a + j
                if m == 0 and n >= ACCS and n - L3A not in range(ACCS):
                    pe.wait_ge(res_read, i * RES + n - ACCS + 1)
                width = D if a in (L2, L3B) else RW
                last = three(ps[:, j % ACCS, 0:width], a_hi[:, m, blk(j)], a_lo[:, m, blk(j)],
                             r_hi[k][:, m, 0:width], r_lo[k][:, m, 0:width], m == 0, m == NB - 1)
                if m == NB - 1:
                    last.then_inc(res_done, 1)

            def group(i, a, m):
                if a == L3B:
                    pe.wait_ge(glo_late_done, i * BPC + m - BPC + 1)
                else:
                    pe.wait_ge(rlo_done, i * LNS + a + m + 1)
                for j in range(BPC):
                    agg(i, a, m, j)

            def single(i, a, j):
                for m in range(NB):
                    agg(i, a, m, j)

            def score(i, t):
                c, m = divmod(t, NB)
                if t == 0:
                    pe.wait_ge(tlo_done, i * 4 + 4)
                if t >= 2:
                    pe.wait_ge(exp_done, i * NT + t - 1)
                for db in range(FB):
                    last = three(ps[:, S_BANK + t % 2], t_hi[:, db, blk(m)], t_lo[:, db, blk(m)],
                                 ht_hi[:, db, chunk(c)], ht_lo[:, db, chunk(c)], db == 0, db == FB - 1)
                last.then_inc(s_done, 1)

            def weigh(i, t):
                c, m = divmod(t, NB)
                pe.wait_ge(plo_done, i * NT + t + 1)
                if t < NB:
                    pe.wait_ge(rlo_done, i * LNS + t + 1)
                for j in range(BPC):
                    n = c * BPC + j
                    if m == 0 and n >= ACCS:
                        pe.wait_ge(res_read, i * RES + n - ACCS + 1)
                    last = three(ps[:, j, 0:RW], p_hi[:, t % RING, blk(j)], p_lo[:, t % RING, blk(j)],
                                 r_hi[0][:, m], r_lo[0][:, m], m == 0, m == NB - 1)
                    if m == NB - 1:
                        last.then_inc(res_done, 1)
                    elif j == BPC - 1:
                        last.then_inc(pv_done, 1)

            def run(i, l, a, order):
                f = {L0: L1, L1: L2, L3B: L3B}.get(a)
                for what, j in order.split():
                    j = int(j)
                    if what == "T":
                        tr(i, l, j)
                    elif what == "J":
                        pj(i, l, j)
                    elif what == "O":
                        single(i, a, j)
                    elif what == "F":
                        group(i, f, j)
                    elif what == "I":
                        si_row(i, j)
                    elif what == "G":
                        gh(i, j)
                    elif what == "t":
                        t_product(i, l, j)
                    elif what == "V":
                        weighed(i, j)
                    else:
                        early(i, f, j)

            def early(i, a, j):
                if j == 0:
                    if a == L3B:
                        pe.wait_ge(glo_done, i * BPC + BPC)
                    else:
                        pe.wait_ge(rlo_done, i * LNS + a + BPC)
                        pe.wait_ge(alo_done, i * NV + NV)
                for m in range(BPC):
                    agg(i, a, m, j)

            def t_product(i, l, v):
                db, c = v // 2, v % 2
                pe.wait_ge(htlo_done, i * LNS + l * NB + NB)
                if v >= 2:
                    pe.wait_ge(tlo_done, i * 4 + l + v - 1)
                for fb in range(FB):
                    last = three(ps[:, T_BANKS[v]], wm[0][:, fb, blk(db)], wm[1][:, fb, blk(db)],
                                 ht_hi[:, fb, chunk(c)], ht_lo[:, fb, chunk(c)], fb == 0, fb == FB - 1)
                last.then_inc(tp_done, 1)

            def si_row(i, j):
                c = j // BPC
                pe.wait_ge(r3_done, i * NB + j + 1)
                if j % BPC == 0:
                    pe.wait_ge(res_read, i * RES + L2 + BPC + SI_BANKS[c] + 1)
                nc.tensor.transpose(ps[:, SI_BANKS[c], blk(j % BPC)],
                                    r3[:, j % R3_RING, D + 1:D + 2].broadcast_to([P, P]),
                                    ident[:]).then_inc(si_done, 1)

            def gh(i, k):
                if k < 2:
                    pe.wait_ge(res_read, i * RES + L2 + BPC + GH_BANKS[k] + 1)
                elif k in (2, 4):
                    pe.wait_ge(htlo_done, i * LNS + LNS + k // 2 - 2)
                elif k in (3, 5):
                    pe.wait_ge(rhi_done, i * LNS + LNS + k // 2 - 2)
                else:
                    pe.wait_ge(g1_done, i * NB + k - 3)
                for fb in range(FB):
                    last = three(ps[:, GH_BANKS[k]], ht_hi[:, fb, blk(k)], ht_lo[:, fb, blk(k)],
                                 wk10[0][:, fb], wk10[1][:, fb], fb == 0, fb == FB - 1)
                last.then_inc(gh_done, 1)

            def weighed(i, v):
                c = v // (NB // 2)
                if v == 0:
                    pe.wait_ge(g1_done, i * NB + 2)
                    pe.wait_ge(si_read, i * 4 + 4)
                    pe.wait_ge(rlo_done, i * LNS + LNS)
                pe.wait_ge(wlo_done, i * NV + v + 1)
                for m in range(2 * v % NB, 2 * v % NB + 2):
                    for j in range(c * BPC, (c + 1) * BPC):
                        agg(i, L3A, m, j)

            AFTER = {10: [(tr, 0)], 11: [(tr, 1), (pj, 0)], 12: [(tr, 2), (pj, 1)],
                     13: [(tr, 3), (pj, 2)], 14: [(pj, 3)]}
            for j in range(NB):
                tr(0, 0, j)
            pe.wait_ge(setup_v, SETUP_T)
            for v in range(4):
                t_product(0, 0, v)
            pe.wait_ge(setup_p, 3 + 1)
            with pe.Fori(0, B) as i:
                pj(i, 0, 0)
                pj(i, 0, 1)
                score(i, 0)
                score(i, 1)
                pj(i, 0, 2)
                pj(i, 0, 3)
                for t in range(NT):
                    if t + 2 < NT:
                        score(i, t + 2)
                    if t < 4:
                        pj(i, 0, t + 4)
                    weigh(i, t)
                    for what, j in AFTER.get(t, ()):
                        what(i, 1, j)
                run(i, 1, L0, TAIL_PE)
                run(i, 2, L1, BLOCKS_PE)
                run(i, 3, L2, WEIGHTS_PE)

                pe.wait_ge(g1_done, i * NB + NB)
                pe.wait_ge(si_read, i * 4 + 4)
                run(i, NEXT, L3B, LAST_PE)


def kernel(x, adj, L0_gnn_Wq_w, L0_gnn_Wq_b, L0_gnn_Wk_w, L0_gnn_Wk_b, L0_gnn_Wv_w, L0_gnn_Wv_b,
           L1_gnn_w, L2_gnn_W, L3_gnn_Wv, L3_gnn_bv, L3_gnn_aw, L3_gnn_ab, L3_gnn_Wk, L3_gnn_bk):
    import numpy as np
    import concourse.bacc as bacc
    from concourse.bass_utils import run_bass_kernel_spmd

    def col(v):
        return np.asarray(v).reshape(-1, P).T

    def row(v):
        return np.asarray(v).reshape(1, -1)

    Wk, W2 = np.asarray(L3_gnn_Wk), np.asarray(L2_gnn_W)
    arrays = {
        "x": x,
        "adjT": np.asarray(adj).transpose(0, 2, 1),
        "wq": L0_gnn_Wq_w, "wk": L0_gnn_Wk_w,
        "bq": col(L0_gnn_Wq_b), "bk": col(L0_gnn_Wk_b),
        "wvT": np.asarray(L0_gnn_Wv_w).T, "bv": row(L0_gnn_Wv_b),
        "w1": L1_gnn_w,
        "w2": np.concatenate([W2[:, D:].T, W2[:, :D].T], axis=1),
        "wv3T": np.asarray(L3_gnn_Wv).T, "bv3": col(L3_gnn_bv),
        "aw": np.asarray(L3_gnn_aw).reshape(2, FB, P).transpose(2, 0, 1), "ab": row(L3_gnn_ab),
        "wk2": Wk[2], "wk10": np.concatenate([Wk[1], Wk[0]], axis=1),
        "bk3": L3_gnn_bk,
    }
    nc = bacc.Bacc("TRN2", target_bir_lowering=False, num_devices=1)
    arrays = {f"{n}_dram": np.ascontiguousarray(a) for n, a in arrays.items()}
    args = [nc.dram_tensor(n, a.shape, mybir.dt.from_np(a.dtype), kind="ExternalInput").ap()
            for n, a in arrays.items()]
    out = nc.dram_tensor("out_dram", (B, N, D), F32, kind="ExternalOutput").ap()
    gnn_program(nc, *args, out)
    r = run_bass_kernel_spmd(nc, [arrays], core_ids=[0])
    return r.results[0]["out_dram"]
```
